# Optimizing a Trainium2 kernel written in Bass

```python
import numpy as np
import jax
import jax.numpy as jnp

def _softmax(x, axis=-1):
    return jax.nn.softmax(x, axis=axis)

def _gelu(x):
    return jax.nn.gelu(x, approximate=True)

def _silu(x):
    return jax.nn.silu(x)

def _sigmoid(x):
    return jax.nn.sigmoid(x)

def _layernorm(x, axis=-1, eps=1e-05):
    m = jnp.mean(x, axis=axis, keepdims=True)
    v = jnp.var(x, axis=axis, keepdims=True)
    return (x - m) / jnp.sqrt(v + eps)

def _scatter_add(tgt, idx, src, axis=0):
    return tgt.at[idx].add(src)

def _segment_sum(src, seg, n):
    return jax.ops.segment_sum(src, seg, n)
kernel_name = 'mk_perceiver_d1_seqx_r8_0c5f5b'

def setup_inputs(seed: int=0):
    np.random.seed(seed)
    _w = jnp.asarray

    def _rec_inputs():
        import jax
        import jax.numpy as jnp
        _rk = jax.random.key(seed)
        x = 7.22e-05 + 1 * jax.random.normal(jax.random.fold_in(_rk, 1), (4, 32, 256), jnp.float32)
        _lenS = 32 - jax.random.randint(jax.random.fold_in(_rk, 7), (4,), 0, max(1, 32 // 4) + 1, jnp.int32)
        _lenS2 = 512 - jax.random.randint(jax.random.fold_in(_rk, 8), (4,), 0, max(1, 512 // 4) + 1, jnp.int32)
        _ctx_512P = jax.random.normal(jax.random.fold_in(_rk, 11), (4, 16, 64), jnp.float32)
        _ctx_512c = jax.random.dirichlet(jax.random.fold_in(_rk, 511), 0.3 * jnp.ones((16,), jnp.float32), (4, 512))
        _ctx_512t = jnp.einsum('bsk,bkd->bsd', _ctx_512c, _ctx_512P)
        _ctx_512t = _ctx_512t * jax.lax.rsqrt(jnp.mean(jnp.square(_ctx_512t)) + 1e-12) * 0.953939
        ctx_512 = -0.000514642 + 1.00011 * (_ctx_512t + 0.3 * jax.random.normal(jax.random.fold_in(_rk, 611), (4, 512, 64), jnp.float32))
        return (x, ctx_512)
    x, ctx_512 = _rec_inputs()

    def _L0_xattn_setup():
        import jax, jax.numpy as jnp
        import numpy as np
        B, S, H, NH, L = (2, 256, 256, 16, 64)
        HD = H // NH
        key = jax.random.key(seed)
        k1, k2, k3, k4, k5 = jax.random.split(key, 5)
        scale = 0.02
        return {'q': jax.random.normal(k1, (B, S, H), dtype=jnp.float32), 'latent_kv': jax.random.normal(k2, (B, S, L), dtype=jnp.float32), 'Wq': jax.random.normal(k3, (H, H), dtype=jnp.float32) * scale, 'Wkv_expand': jax.random.normal(k4, (2 * H, L), dtype=jnp.float32) * scale, 'Wout': jax.random.normal(k5, (H, H), dtype=jnp.float32) * scale}
    _L0_xattn_all = _L0_xattn_setup()
    _L0_xattn_in = {k: v for k, v in _L0_xattn_all.items() if k in ('Wq', 'Wkv_expand', 'Wout')}
    del _L0_xattn_all

    def _L0_attn_setup():
        import jax, jax.numpy as jnp
        import numpy as np
        DIM = 256
        HEADS = 16
        HEAD_DIM = DIM // HEADS
        RANK = 16
        ALPHA = 8.0
        SCALING = ALPHA / RANK
        SCALE = HEAD_DIM ** (-0.5)

        def lora_linear(x, W, b, Bm, Am):
            out = jnp.einsum('bld,od->blo', x, W) + b
            upd = jnp.einsum('blr,or->blo', jnp.einsum('bld,rd->blr', x, Bm), Am)
            return out + SCALING * upd

        def _split(t):
            B, L, D = t.shape
            return t.reshape(B, L, HEADS, HEAD_DIM).transpose(0, 2, 1, 3)
        key = jax.random.key(seed)
        ks = jax.random.split(key, 20)
        B, L = (4, 256)
        x = jax.random.normal(ks[0], (B, L, DIM), dtype=jnp.float32)
        s = 0.02
        inp = {'x': x}
        for i, name in enumerate(['q', 'k', 'v', 'o']):
            inp[f'W{name}'] = jax.random.normal(ks[1 + 4 * i], (DIM, DIM), jnp.float32) * s
            inp[f'b{name}'] = jax.random.normal(ks[2 + 4 * i], (DIM,), jnp.float32) * s
            inp[f'B{name}'] = jax.random.normal(ks[3 + 4 * i], (RANK, DIM), jnp.float32) * s
            inp[f'A{name}'] = jax.random.uniform(ks[4 + 4 * i], (DIM, RANK), jnp.float32, -0.1, 0.1)
        return inp
    _L0_attn_all = _L0_attn_setup()
    _L0_attn_in = {k: v for k, v in _L0_attn_all.items() if k in ('Wq', 'bq', 'Bq', 'Aq', 'Wk', 'bk', 'Bk', 'Ak', 'Wv', 'bv', 'Bv', 'Av', 'Wo', 'bo', 'Bo', 'Ao')}
    del _L0_attn_all

    def _L0_ffn_setup():
        import jax, jax.numpy as jnp
        import numpy as np
        B, S, D = (2, 256, 256)
        I = 128
        E = 32
        K = 4
        NS = 1
        ALPHA = 7.0

        def _clamped_swiglu(x, wg, wu, wd):
            g = jnp.clip(x @ wg.T, -ALPHA, ALPHA)
            u = jnp.clip(x @ wu.T, -ALPHA, ALPHA)
            return jax.nn.silu(g) * u @ wd.T
        key = jax.random.key(seed)
        ks = jax.random.split(key, 9)
        s = 0.02
        return {'hidden': jax.random.normal(ks[0], (B, S, D), jnp.float32), 'router_w': jax.random.normal(ks[1], (E, D), jnp.float32) * s, 'expert_bias': jax.random.normal(ks[2], (E,), jnp.float32) * s, 'gate_w': jax.random.normal(ks[3], (E, I, D), jnp.float32) * s, 'up_w': jax.random.normal(ks[4], (E, I, D), jnp.float32) * s, 'down_w': jax.random.normal(ks[5], (E, D, I), jnp.float32) * s, 'shared_gate_w': jax.random.normal(ks[6], (NS * I, D), jnp.float32) * s, 'shared_up_w': jax.random.normal(ks[7], (NS * I, D), jnp.float32) * s, 'shared_down_w': jax.random.normal(ks[8], (D, NS * I), jnp.float32) * s}
    _L0_ffn_all = _L0_ffn_setup()
    _L0_ffn_in = {k: v for k, v in _L0_ffn_all.items() if k in ('router_w', 'expert_bias', 'gate_w', 'up_w', 'down_w', 'shared_gate_w', 'shared_up_w', 'shared_down_w')}
    del _L0_ffn_all
    return {'x': x, 'ctx_512': ctx_512, 'L0_xattn_Wq': _L0_xattn_in['Wq'], 'L0_xattn_Wkv_expand': _L0_xattn_in['Wkv_expand'], 'L0_xattn_Wout': _L0_xattn_in['Wout'], 'L0_attn_Wq': _L0_attn_in['Wq'], 'L0_attn_bq': _L0_attn_in['bq'], 'L0_attn_Bq': _L0_attn_in['Bq'], 'L0_attn_Aq': _L0_attn_in['Aq'], 'L0_attn_Wk': _L0_attn_in['Wk'], 'L0_attn_bk': _L0_attn_in['bk'], 'L0_attn_Bk': _L0_attn_in['Bk'], 'L0_attn_Ak': _L0_attn_in['Ak'], 'L0_attn_Wv': _L0_attn_in['Wv'], 'L0_attn_bv': _L0_attn_in['bv'], 'L0_attn_Bv': _L0_attn_in['Bv'], 'L0_attn_Av': _L0_attn_in['Av'], 'L0_attn_Wo': _L0_attn_in['Wo'], 'L0_attn_bo': _L0_attn_in['bo'], 'L0_attn_Bo': _L0_attn_in['Bo'], 'L0_attn_Ao': _L0_attn_in['Ao'], 'L0_ffn_router_w': _L0_ffn_in['router_w'], 'L0_ffn_expert_bias': _L0_ffn_in['expert_bias'], 'L0_ffn_gate_w': _L0_ffn_in['gate_w'], 'L0_ffn_up_w': _L0_ffn_in['up_w'], 'L0_ffn_down_w': _L0_ffn_in['down_w'], 'L0_ffn_shared_gate_w': _L0_ffn_in['shared_gate_w'], 'L0_ffn_shared_up_w': _L0_ffn_in['shared_up_w'], 'L0_ffn_shared_down_w': _L0_ffn_in['shared_down_w']}

def reference(x, ctx_512, L0_xattn_Wq, L0_xattn_Wkv_expand, L0_xattn_Wout, L0_attn_Wq, L0_attn_bq, L0_attn_Bq, L0_attn_Aq, L0_attn_Wk, L0_attn_bk, L0_attn_Bk, L0_attn_Ak, L0_attn_Wv, L0_attn_bv, L0_attn_Bv, L0_attn_Av, L0_attn_Wo, L0_attn_bo, L0_attn_Bo, L0_attn_Ao, L0_ffn_router_w, L0_ffn_expert_bias, L0_ffn_gate_w, L0_ffn_up_w, L0_ffn_down_w, L0_ffn_shared_gate_w, L0_ffn_shared_up_w, L0_ffn_shared_down_w):
    import jax
    import jax.numpy as jnp

    def _L0_xattn_ref(q, latent_kv, Wq, Wkv_expand, Wout):
        import jax, jax.numpy as jnp
        import numpy as np
        B, S, H, NH, L = (2, 256, 256, 16, 64)
        HD = H // NH
        b, sq, _ = q.shape
        sk = latent_kv.shape[1]
        qp = q @ Wq.T
        kv = latent_kv @ Wkv_expand.T
        k, v = jnp.split(kv, 2, axis=-1)
        qh = qp.reshape(b, sq, NH, HD).transpose(0, 2, 1, 3)
        kh = k.reshape(b, sk, NH, HD).transpose(0, 2, 1, 3)
        vh = v.reshape(b, sk, NH, HD).transpose(0, 2, 1, 3)
        inv_sqrt_d = 1.0 / jnp.sqrt(jnp.float32(HD))
        scores = jnp.einsum('bhqd,bhkd->bhqk', qh, kh) * inv_sqrt_d
        causal = jnp.tril(jnp.ones((sq, sk), dtype=bool))
        scores = jnp.where(causal, scores, jnp.finfo(scores.dtype).min)
        attn = jax.nn.softmax(scores, axis=-1)
        out = jnp.einsum('bhqk,bhkd->bhqd', attn, vh)
        out = out.transpose(0, 2, 1, 3).reshape(b, sq, H)
        return out @ Wout.T

    def _L0_attn_ref(x, Wq, bq, Bq, Aq, Wk, bk, Bk, Ak, Wv, bv, Bv, Av, Wo, bo, Bo, Ao):
        import jax, jax.numpy as jnp
        import numpy as np
        DIM = 256
        HEADS = 16
        HEAD_DIM = DIM // HEADS
        RANK = 16
        ALPHA = 8.0
        SCALING = ALPHA / RANK
        SCALE = HEAD_DIM ** (-0.5)

        def lora_linear(x, W, b, Bm, Am):
            out = jnp.einsum('bld,od->blo', x, W) + b
            upd = jnp.einsum('blr,or->blo', jnp.einsum('bld,rd->blr', x, Bm), Am)
            return out + SCALING * upd

        def _split(t):
            B, L, D = t.shape
            return t.reshape(B, L, HEADS, HEAD_DIM).transpose(0, 2, 1, 3)
        q = _split(lora_linear(x, Wq, bq, Bq, Aq))
        k = _split(lora_linear(x, Wk, bk, Bk, Ak))
        v = _split(lora_linear(x, Wv, bv, Bv, Av))
        scores = jnp.einsum('bhqd,bhkd->bhqk', q, k) * SCALE
        attn = jax.nn.softmax(scores, axis=-1)
        out = jnp.einsum('bhqk,bhkd->bhqd', attn, v)
        B, H, L, hd = out.shape
        out = out.transpose(0, 2, 1, 3).reshape(B, L, H * hd)
        return lora_linear(out, Wo, bo, Bo, Ao)

    def _L0_ffn_ref(hidden, router_w, expert_bias, gate_w, up_w, down_w, shared_gate_w, shared_up_w, shared_down_w):
        import jax, jax.numpy as jnp
        import numpy as np
        B, S, D = (2, 256, 256)
        I = 128
        E = 32
        K = 4
        NS = 1
        ALPHA = 7.0

        def _clamped_swiglu(x, wg, wu, wd):
            g = jnp.clip(x @ wg.T, -ALPHA, ALPHA)
            u = jnp.clip(x @ wu.T, -ALPHA, ALPHA)
            return jax.nn.silu(g) * u @ wd.T
        Bb, Ss, Dd = hidden.shape
        flat = hidden.reshape(-1, Dd)
        T = flat.shape[0]
        logits = flat @ router_w.T
        scores = jnp.sqrt(jax.nn.softplus(logits))
        _, idx = jax.lax.top_k(scores + expert_bias, K)
        topv = jnp.take_along_axis(scores, idx, axis=1)
        topv = topv / (topv.sum(axis=-1, keepdims=True) + 1e-20)
        probs = jnp.zeros((T, E), flat.dtype).at[jnp.arange(T)[:, None], idx].set(topv)

        def body(acc, xs):
            wg, wu, wd, p = xs
            return (acc + p[:, None] * _clamped_swiglu(flat, wg, wu, wd), None)
        out, _ = jax.lax.scan(body, jnp.zeros_like(flat), (gate_w, up_w, down_w, probs.T))
        out = out + _clamped_swiglu(flat, shared_gate_w, shared_up_w, shared_down_w)
        return out.reshape(Bb, Ss, Dd)
    x = x + _L0_xattn_ref(_layernorm(x, axis=-1), ctx_512, L0_xattn_Wq, L0_xattn_Wkv_expand, L0_xattn_Wout)
    x = x + _L0_attn_ref(_layernorm(x, axis=-1), L0_attn_Wq, L0_attn_bq, L0_attn_Bq, L0_attn_Aq, L0_attn_Wk, L0_attn_bk, L0_attn_Bk, L0_attn_Ak, L0_attn_Wv, L0_attn_bv, L0_attn_Bv, L0_attn_Av, L0_attn_Wo, L0_attn_bo, L0_attn_Bo, L0_attn_Ao)
    x = x + _L0_ffn_ref(_layernorm(x, axis=-1), L0_ffn_router_w, L0_ffn_expert_bias, L0_ffn_gate_w, L0_ffn_up_w, L0_ffn_down_w, L0_ffn_shared_gate_w, L0_ffn_shared_up_w, L0_ffn_shared_down_w)
    return x

_drawn_inputs = setup_inputs


def setup_inputs(seed=0):
    import zlib

    import numpy as np

    out = dict(_drawn_inputs(seed))
    spreads = {}
    factors = {'L0_xattn_Wq': 8.0,
     'L0_attn_Wq': 8.0,
     'L0_attn_bq': 8.0,
     'L0_attn_Bq': 8.0,
     'L0_attn_Aq': 8.0,
     'L0_attn_Wk': 8.0,
     'L0_attn_bk': 8.0,
     'L0_attn_Bk': 8.0,
     'L0_attn_Ak': 8.0,
     'L0_attn_Wv': 3.165,
     'L0_attn_bv': 8.0,
     'L0_attn_Bv': 8.0,
     'L0_attn_Av': 8.0,
     'L0_attn_Wo': 2.861,
     'L0_attn_bo': 2.923,
     'L0_attn_Bo': 8.0,
     'L0_attn_Ao': 8.0,
     'L0_ffn_router_w': 8.0,
     'L0_ffn_expert_bias': 8.0,
     'L0_ffn_gate_w': 8.0,
     'L0_ffn_up_w': 8.0,
     'L0_ffn_down_w': 8.0,
     'L0_ffn_shared_gate_w': 4.934,
     'L0_ffn_shared_up_w': 4.82,
     'L0_ffn_shared_down_w': 4.876}
    for name, (base, spread) in spreads.items():
        noise = np.random.default_rng([zlib.crc32(name.encode()), seed]).standard_normal(out[name].shape)
        drawn = base * np.exp(spread * noise) if base else spread * noise
        out[name] = jnp.asarray(drawn.astype(out[name].dtype))
    for name, factor in factors.items():
        out[name] = (out[name] * factor).astype(out[name].dtype)
    return out
```

```python
from contextlib import ExitStack

import concourse.bass as bass
from concourse import mybir

F32 = mybir.dt.float32
BF16 = mybir.dt.bfloat16
ALU = mybir.AluOpType
ACT = mybir.ActivationFunctionType
AX_X = mybir.AxisListType.X

B, S, D, L = 4, 32, 256, 64
T = B * S
DC = D // 128
NH, HD = 16, 16
HC = NH // DC
R = 16
LORA_SCALE = 8.0 / R
SM_SCALE = HD ** -0.5
E, I, K = 32, 128, 4
CLIP = 7.0
EPS = 1e-5
PAIRS = E // 2
GU = 4 * I
SENTINEL = 3e38
TINY = 1e-30

IDENT, HMASK, BIASQ, BIASK, EBIAS, ROUTER = 0, 128, 136, 138, 140, 172
SMALL = ROUTER + DC * E
CTX, WKV = 0, T
ONES, BV, BO = 0, T, T + D


def build(nc, x, small, causal, ctx_kv, x_wq, x_wo, lora, rows, attn_w, shared_w, moe_w, out):
    with ExitStack() as ctx:
        def sb(name, shape, dt=F32):
            return ctx.enter_context(nc.sbuf_tensor(name, shape, dt))

        def pb(name):
            return ctx.enter_context(nc.psum_tensor(name, [128, 512], F32))

        def sem(name):
            return ctx.enter_context(nc.semaphore(name))

        x_sb = sb("x_sb", [T, D])
        small_sb = sb("small_sb", [128, SMALL])
        causal_sb = sb("causal_sb", [128, 128 + HC * S], BF16)
        ctx_sb = sb("ctx_sb", [L, T + 2 * D])
        xwq_sb = sb("xwq_sb", [128, DC, D])
        xwo_sb = sb("xwo_sb", [128, DC, D])
        lora_sb = sb("lora_sb", [R, 2, 4, D])
        rows_sb = sb("rows_sb", [1, T + 2 * D])
        aw_sb = sb("aw_sb", [128, 4, DC * D])
        shared_sb = sb("shared_sb", [128, DC * 2 * I + D])
        gu_w = sb("gu_w", [128, PAIRS * DC * GU])
        dn_w = sb("dn_w", [128, PAIRS * 2 * D])

        ident = small_sb[:, IDENT:IDENT + 128]
        hmask = small_sb[:, HMASK:HMASK + HC]

        lora_half = sb("lora_half", [128, 2, DC * D])
        stats = sb("stats", [T, 3, 6])
        moments = sb("moments", [T, 3, 2])
        var_eps = sb("var_eps", [T, 3])
        rstd = sb("rstd", [T, 3])
        inv_sqrt_power = sb("inv_sqrt_power", [T, 1])
        sqrt_power = sb("sqrt_power", [T, E])
        xn = sb("xn", [T, 3, D])
        xnT = sb("xnT", [128, 3, DC, T])
        qT = sb("qT", [128, 2, DC, T])
        k_heads = sb("k_heads", [128, 2, DC, HC, T])
        v_ones = sb("v_ones", [T, 2, NH, HD + 1])
        row_max = sb("row_max", [T, 2, NH])
        shifted = sb("shifted", [T, NH * S])
        probs = sb("probs", [T, NH * S])
        probsT = sb("probsT", [T, NH, T])
        inv_sum = sb("inv_sum", [T, 2, NH])
        heads_out = sb("heads_out", [T, 2, D])
        heads_outT = sb("heads_outT", [128, 2, DC, T])
        x1 = sb("x1", [T, D])
        x2 = sb("x2", [T, D])
        abs_logits = sb("abs_logits", [T, E])
        e_abs = sb("e_abs", [T, E])
        one_plus = sb("one_plus", [T, E])
        ln_one_plus = sb("ln_one_plus", [T, E])
        den = sb("den", [T, E])
        ratio = sb("ratio", [T, E])
        softplus = sb("softplus", [T, E])
        score = sb("score", [T, E])
        key = sb("key", [T, E + K])
        top8 = sb("top8", [T, 8])
        replaced = sb("replaced", [T, E + K])
        chosen = sb("chosen", [T, E])
        weight = sb("weight", [T, E])
        weight_sum = sb("weight_sum", [T, 2])
        gate = sb("gate", [T, E])
        gu_clip = sb("gu_clip", [T, 2, 2, 2, I])
        silu = sb("silu", [T, 2, 2, I])
        h = sb("h", [T, 2, 2, I])
        hT = sb("hT", [128, 2, 2, T])
        y_sb = sb("y_sb", [T, D])

        bK, bV, bT, bQ, bS0, bS1, bO, bY = (pb(n) for n in ("bK", "bV", "bT", "bQ", "bS0", "bS1", "bO", "bY"))
        bS = (bS0, bS1)

        ld = {n: sem("ld_" + n) for n in ("x", "small", "causal", "ctx", "xwq", "xwo", "lora", "rows",
                                          "aw", "shared")}
        ld_gu = [sem(f"ld_gu{j}") for j in range(2)]
        ld_dn = [sem(f"ld_dn{j}") for j in range(2)]
        zeroed = sem("zeroed")
        ln_step = sem("ln_step")
        var_ready = sem("var_ready")
        rstd_ready = sem("rstd_ready")
        softplus_ready = sem("softplus_ready")
        score_ready = sem("score_ready")
        powers_set = sem("powers_set")
        xn_ready = sem("xn_ready")
        xnT_psum = sem("xnT_psum")
        xnT_ready = sem("xnT_ready")
        k_psum = sem("k_psum")
        v_psum = sem("v_psum")
        q_psum = sem("q_psum")
        k_ready = sem("k_ready")
        v_ready = sem("v_ready")
        q_ready = sem("q_ready")
        lora_psum = sem("lora_psum")
        lora_scaled = sem("lora_scaled")
        lora_merged = sem("lora_merged")
        scores_ready = sem("scores_ready")
        max_ready = sem("max_ready")
        shift_ready = sem("shift_ready")
        exp_ready = sem("exp_ready")
        probsT_ready = sem("probsT_ready")
        pv_ready = sem("pv_ready")
        inv_ready = sem("inv_ready")
        heads_ready = sem("heads_ready")
        headsT_psum = sem("headsT_psum")
        headsT_ready = sem("headsT_ready")
        y_psum = sem("y_psum")
        x_ready = sem("x_ready")
        logits_ready = sem("logits_ready")
        abs_ready = sem("abs_ready")
        e_abs_ready = sem("e_abs_ready")
        one_plus_ready = sem("one_plus_ready")
        ln_ready = sem("ln_ready")
        route_step = sem("route_step")
        gate_ready = sem("gate_ready")
        gu_ready = sem("gu_ready")
        clip_ready = sem("clip_ready")
        silu_ready = sem("silu_ready")
        h_ready = sem("h_ready")
        hT_psum = sem("hT_psum")
        hT_ready = sem("hT_ready")
        y_done = sem("y_done")
        fin = sem("fin")
        stored = sem("stored")

        block = ctx.enter_context(nc.Block())

        @block.sync
        def _(sp):
            for name, dst, src in (("x", x_sb, x), ("small", small_sb, small), ("ctx", ctx_sb, ctx_kv),
                                   ("xwq", xwq_sb, x_wq), ("causal", causal_sb, causal), ("lora", lora_sb, lora),
                                   ("aw", aw_sb, attn_w), ("xwo", xwo_sb, x_wo), ("rows", rows_sb, rows),
                                   ("shared", shared_sb, shared_w)):
                sp.dma_start(dst[:], src).then_inc(ld[name], 16)

            def load_pair(p, j):
                nc.sync.dma_start(gu_w[:, bass.ts(p, DC * GU)], moe_w[:, bass.ds(p * (DC * GU + 2 * D), DC * GU)]
                                  ).then_inc(ld_gu[j], 16)
                nc.sync.dma_start(dn_w[:, bass.ts(p, 2 * D)],
                                  moe_w[:, bass.ds(p * (DC * GU + 2 * D) + DC * GU, 2 * D)]).then_inc(ld_dn[j], 16)

            for j in range(2):
                load_pair(j, j)
            with nc.sync.Fori(1, PAIRS // 2) as i:
                for j in range(2):
                    sp.wait_ge(ld_gu[j], i * 16)
                    sp.wait_ge(ld_dn[j], i * 16)
                    load_pair(i * 2 + j, j)
            sp.wait_ge(fin, 1)
            sp.dma_start(out, y_sb[:]).then_inc(stored, 16)
            sp.wait_ge(stored, 16)

        @block.gpsimd
        def _(pool):
            nc.gpsimd.memset(inv_sqrt_power[:], -0.5).then_inc(powers_set, 1)
            nc.gpsimd.memset(sqrt_power[:], 0.5).then_inc(powers_set, 1)
            pool.wait_ge(powers_set, 2)

            def inverse_sqrt(n):
                pool.wait_ge(var_ready, n + 1)
                nc.gpsimd.tensor_tensor(rstd[:, n:n + 1], var_eps[:, n:n + 1], inv_sqrt_power[:], ALU.pow
                                        ).then_inc(rstd_ready, 1)

            inverse_sqrt(0)
            nc.gpsimd.memset(probsT[:], 0.0).then_inc(zeroed, 1)
            nc.gpsimd.memset(v_ones[:], 1.0).then_inc(zeroed, 1)
            nc.gpsimd.memset(key[:, E:E + K], SENTINEL).then_inc(zeroed, 1)
            pool.wait_ge(ld["aw"], 16)
            for m in range(4):
                pool.wait_ge(lora_scaled, m + 1)
                nc.gpsimd.tensor_tensor(aw_sb[:, m], aw_sb[:, m], lora_half[:, m % 2], ALU.add
                                        ).then_inc(lora_merged, 1)
            inverse_sqrt(1)
            inverse_sqrt(2)
            pool.wait_ge(softplus_ready, 1)
            nc.gpsimd.tensor_tensor(score[:], softplus[:], sqrt_power[:], ALU.pow).then_inc(score_ready, 1)

        @block.tensor
        def _(pe):
            def merge_lora(m, bank):
                for c in range(DC):
                    last = nc.tensor.matmul(bank[:, c * D:(c + 1) * D], lora_sb[:, 0, m, c * 128:(c + 1) * 128],
                                            lora_sb[:, 1, m, :], start=True, stop=True)
                last.then_inc(lora_psum, 1)

            def transpose_xn(n):
                pe.wait_ge(xn_ready, n + 1)
                for c in range(DC):
                    last = nc.tensor.transpose(bT[:, c * T:(c + 1) * T], xn[:, n, c * 128:(c + 1) * 128], ident)
                last.then_inc(xnT_psum, 1)
                pe.wait_ge(xnT_ready, n + 1)

            def project_T(bank, w, a, done):
                for c in range(DC):
                    for k in range(DC):
                        last = nc.tensor.matmul(bank[:, c * T:(c + 1) * T], w[:, k, c * 128:(c + 1) * 128],
                                                xnT[:, a, k, :], start=(k == 0), stop=(k == DC - 1))
                last.then_inc(done, 1)

            def scores(a, c):
                if c == 0:
                    pe.wait_ge(q_ready, a + 1)
                pe.wait_ge(k_ready, DC * a + c + 1)
                if a == 0:
                    nc.tensor.matmul(bS[c][:, 0:HC * S], causal_sb[:, 0:128], causal_sb[:, 128:],
                                     start=True, stop=False, skip_group_check=True)
                for b in range(B):
                    last = nc.tensor.matmul(bS[c][b * S:(b + 1) * S, 0:HC * S], qT[:, a, c, b * S:(b + 1) * S],
                                            k_heads[:, a, c, :, b * S:(b + 1) * S], start=(a == 1), stop=True,
                                            skip_group_check=True)
                last.then_inc(scores_ready, 1)

            def attend(a, c):
                pe.wait_ge(probsT_ready, DC * a + c + 1)
                if c == 0:
                    pe.wait_ge(v_ready, a + 1)
                for n in range(c * HC, (c + 1) * HC):
                    last = nc.tensor.matmul(bO[:, n * (HD + 1):(n + 1) * (HD + 1)], probsT[:, n, :],
                                            v_ones[:, a, n, :], start=True, stop=True)
                last.then_inc(pv_ready, 1)

            def project_out(a, w):
                pe.wait_ge(heads_ready, a + 1)
                for c in range(DC):
                    last = nc.tensor.transpose(bT[:, c * T:(c + 1) * T], heads_out[:, a, c * 128:(c + 1) * 128], ident)
                last.then_inc(headsT_psum, 1)
                pe.wait_ge(headsT_ready, a + 1)
                for c in range(DC):
                    last = nc.tensor.matmul(bY[:, 0:D], heads_outT[:, a, c, :], w[:, c, :],
                                            start=(a == 0 and c == 0), stop=(c == DC - 1))
                last.then_inc(y_psum, 1)

            pe.wait_ge(ld["ctx"], 16)
            for c in range(DC):
                last = nc.tensor.matmul(bK[:, c * T:(c + 1) * T], ctx_sb[:, WKV + c * 128:WKV + (c + 1) * 128],
                                        ctx_sb[:, CTX:CTX + T], start=True, stop=True)
            last.then_inc(k_psum, 1)
            nc.tensor.matmul(bV[:, 0:D], ctx_sb[:, CTX:CTX + T], ctx_sb[:, WKV + D:WKV + 2 * D],
                             start=True, stop=True).then_inc(v_psum, 1)
            pe.wait_ge(ld["small"], 16)
            transpose_xn(0)
            pe.wait_ge(ld["xwq"], 16)
            project_T(bQ, xwq_sb, 0, q_psum)
            pe.wait_ge(ld["causal"], 16)
            scores(0, 0)
            scores(0, 1)
            pe.wait_ge(ld["lora"], 16)
            merge_lora(0, bY)
            pe.wait_ge(k_ready, 2)
            merge_lora(1, bK)
            attend(0, 0)
            pe.wait_ge(v_ready, 1)
            merge_lora(2, bV)
            attend(0, 1)
            pe.wait_ge(q_ready, 1)
            merge_lora(3, bQ)
            pe.wait_ge(ld["xwo"], 16)
            pe.wait_ge(lora_scaled, 1)
            project_out(0, xwo_sb)

            pe.wait_ge(lora_scaled, 3)
            pe.wait_ge(ld["rows"], 16)
            nc.tensor.matmul(bV[:, 0:D], rows_sb[:, ONES:ONES + T], rows_sb[:, BV:BV + D], start=True, stop=False)
            transpose_xn(1)
            aw = [aw_sb[:, m].rearrange("p (c n) -> p c n", c=DC) for m in range(4)]
            pe.wait_ge(lora_merged, 2)
            project_T(bK, aw[1], 1, k_psum)
            pe.wait_ge(lora_scaled, 4)
            project_T(bQ, aw[0], 1, q_psum)
            pe.wait_ge(lora_merged, 4)
            for k in range(DC):
                last = nc.tensor.matmul(bV[:, 0:D], xnT[:, 1, k, :], aw[2][:, k, :], start=False, stop=(k == DC - 1))
            last.then_inc(v_psum, 1)
            scores(1, 0)
            scores(1, 1)
            pe.wait_ge(x_ready, 1)
            nc.tensor.matmul(bY[:, 0:D], rows_sb[:, ONES:ONES + T], rows_sb[:, BO:BO + D], start=True, stop=False)
            attend(1, 0)
            attend(1, 1)
            project_out(1, aw[3])

            transpose_xn(2)
            for k in range(DC):
                last = nc.tensor.matmul(bQ[:, 0:E], xnT[:, 2, k, :], small_sb[:, ROUTER + k * E:ROUTER + (k + 1) * E],
                                        start=(k == 0), stop=(k == DC - 1))
            last.then_inc(logits_ready, 1)

            def gate_up(n, j, visit):
                pe.wait_ge(ld_gu[1 - j], visit * 16)
                pe.wait_ge(clip_ready, n - 1)
                for k in range(DC):
                    last = nc.tensor.matmul(bS[j][:, 0:GU], xnT[:, 2, k, :],
                                            gu_w[:, bass.ds((n - 1) * (DC * GU) + k * GU, GU)],
                                            start=(k == 0), stop=(k == DC - 1))
                last.then_inc(gu_ready, 1)

            def transpose_h(n, j, width=2):
                pe.wait_ge(h_ready, n + 1)
                for e in range(width):
                    last = nc.tensor.transpose((bK, bV)[j][:, e * T:(e + 1) * T], h[:, j, e, :], ident)
                last.then_inc(hT_psum, 1)

            def down(n, j, visit, stop=False):
                pe.wait_ge(ld_dn[1 - j], visit * 16)
                pe.wait_ge(hT_ready, n + 1)
                for e in range(2):
                    last = nc.tensor.matmul(bO[:, 0:D], hT[:, j, e, :],
                                            dn_w[:, bass.ds((n - 1) * (2 * D) + e * D, D)],
                                            start=False, stop=(stop and e == 1), skip_group_check=True)
                last.then_inc(y_done, 1)

            pe.wait_ge(ld["shared"], 16)
            for k in range(DC):
                last = nc.tensor.matmul(bS[0][:, 0:2 * I], xnT[:, 2, k, :], shared_sb[:, k * 2 * I:(k + 1) * 2 * I],
                                        start=(k == 0), stop=(k == DC - 1))
            last.then_inc(gu_ready, 1)
            pe.wait_ge(ld_gu[0], 16)
            for k in range(DC):
                last = nc.tensor.matmul(bS[1][:, 0:GU], xnT[:, 2, k, :], gu_w[:, k * GU:(k + 1) * GU],
                                        start=(k == 0), stop=(k == DC - 1))
            last.then_inc(gu_ready, 1)
            transpose_h(0, 0, width=1)
            gate_up(2, 0, 1)
            pe.wait_ge(hT_ready, 1)
            nc.tensor.matmul(bO[:, 0:D], hT[:, 0, 0, :], shared_sb[:, DC * 2 * I:], start=True, stop=False,
                             skip_group_check=True).then_inc(y_done, 1)
            transpose_h(1, 1)
            with nc.tensor.Fori(0, PAIRS // 2 - 1) as i:
                gate_up(i * 2 + 3, 1, i + 2)
                down(i * 2 + 1, 1, i + 1)
                transpose_h(i * 2 + 2, 0)
                gate_up(i * 2 + 4, 0, i + 2)
                down(i * 2 + 2, 0, i + 1)
                transpose_h(i * 2 + 3, 1)
            down(PAIRS - 1, 1, PAIRS // 2)
            transpose_h(PAIRS, 0)
            down(PAIRS, 0, PAIRS // 2, stop=True)

        @block.scalar
        def _(act):
            nc.scalar.preload_act_table(ACT.Ln)

            def scale_lora(m, bank):
                act.wait_ge(lora_psum, m + 1)
                if m >= 2:
                    act.wait_ge(lora_merged, m - 1)
                nc.scalar.activation(lora_half[:, m % 2], bank[:, :], ACT.Copy, scale=LORA_SCALE
                                     ).then_inc(lora_scaled, 1)

            def exps(a):
                for c in range(DC):
                    act.wait_ge(shift_ready, DC * a + c + 1)
                    half = slice(c * HC * S, (c + 1) * HC * S)
                    nc.scalar.activation(probs[:, half], shifted[:, half], ACT.Exp, scale=SM_SCALE
                                         ).then_inc(exp_ready, 1)

            def copy_xnT(n):
                act.wait_ge(xnT_psum, n + 1)
                nc.scalar.activation(xnT[:, n], bT[:, 0:DC * T], ACT.Copy).then_inc(xnT_ready, 1)

            def copy_v(a):
                act.wait_ge(v_psum, a + 1)
                if a == 0:
                    act.wait_ge(zeroed, 2)
                nc.scalar.activation(v_ones[:, a, :, 0:HD], bV[:, 0:D].rearrange("p (h d) -> p h d", h=NH), ACT.Copy
                                     ).then_inc(v_ready, 1)

            def copy_headsT(a):
                act.wait_ge(headsT_psum, a + 1)
                nc.scalar.activation(heads_outT[:, a], bT[:, 0:DC * T], ACT.Copy).then_inc(headsT_ready, 1)

            copy_v(0)
            copy_xnT(0)
            act.wait_ge(q_psum, 1)
            nc.scalar.activation(qT[:, 0], bQ[:, 0:DC * T], ACT.Copy).then_inc(q_ready, 1)
            exps(0)
            for m, bank in enumerate((bY, bK, bV, bQ)):
                scale_lora(m, bank)
            copy_headsT(0)

            copy_xnT(1)
            act.wait_ge(q_psum, 2)
            for c in range(DC):
                last = nc.scalar.activation(qT[:, 1, c], bQ[:, c * T:(c + 1) * T], ACT.Identity,
                                            bias=small_sb[:, BIASQ + c:BIASQ + c + 1])
            last.then_inc(q_ready, 1)
            copy_v(1)
            exps(1)
            copy_headsT(1)

            copy_xnT(2)
            act.wait_ge(logits_ready, 1)
            nc.scalar.activation(abs_logits[:], bQ[:, 0:E], ACT.Abs).then_inc(abs_ready, 1)
            act.wait_ge(abs_ready, 1)
            nc.scalar.activation(e_abs[:], abs_logits[:], ACT.Exp, scale=-1.0).then_inc(e_abs_ready, 1)
            act.wait_ge(one_plus_ready, 1)
            nc.scalar.activation(ln_one_plus[:], one_plus[:], ACT.Ln).then_inc(ln_ready, 1)
            nc.scalar.preload_act_table(ACT.Silu)

            def unit(n, j, width=2):
                act.wait_ge(clip_ready, n + 1)
                nc.scalar.activation(silu[:, j, 0:width], gu_clip[:, j, 0:width, 0, :], ACT.Silu
                                     ).then_inc(silu_ready, 1)
                act.wait_ge(hT_psum, n + 1)
                nc.scalar.activation(hT[:, j, 0:width], (bK, bV)[j][:, 0:width * T], ACT.Copy).then_inc(hT_ready, 1)

            unit(0, 0, width=1)
            with nc.scalar.Fori(0, PAIRS // 2) as i:
                unit(i * 2 + 1, 1)
                unit(i * 2 + 2, 0)

        @block.vector
        def _(dve):
            links = {"ln": 0, "route": 0}

            def link(ins, which, s):
                links[which] += 1
                ins.then_inc(s, 1)
                dve.wait_ge(s, links[which])

            def layer_norm(n, src):
                link(nc.vector.bn_stats(stats[:, n], src), "ln", ln_step)
                link(nc.vector.bn_aggr(moments[:, n], stats[:, n]), "ln", ln_step)
                nc.vector.tensor_scalar(var_eps[:, n:n + 1], moments[:, n, 1:2], EPS, None, ALU.add
                                        ).then_inc(var_ready, 1)
                dve.wait_ge(rstd_ready, n + 1)
                nc.vector.tensor_scalar(xn[:, n], src, moments[:, n, 0:1], rstd[:, n:n + 1],
                                        ALU.subtract, ALU.mult).then_inc(xn_ready, 1)

            def spread_keys(a, c):
                src = bK[:, c * T:(c + 1) * T].unsqueeze(1).to_broadcast([128, HC, T])
                mask = hmask.unsqueeze(2).to_broadcast([128, HC, T])
                if a == 0:
                    ins = nc.vector.tensor_tensor(k_heads[:, a, c], src, mask, ALU.mult)
                else:
                    ins = nc.vector.scalar_tensor_tensor(k_heads[:, a, c], src, small_sb[:, BIASK + c:BIASK + c + 1],
                                                         mask, ALU.add, ALU.mult)
                ins.then_inc(k_ready, 1)

            def softmax_half(a, c):
                dve.wait_ge(scores_ready, DC * a + c + 1)
                sc = bS[c][:, 0:HC * S].rearrange("p (h k) -> p h k", h=HC)
                mx = row_max[:, a, c * HC:(c + 1) * HC]
                nc.vector.tensor_reduce(mx, sc, AX_X, ALU.max).then_inc(max_ready, 1)
                dve.wait_ge(max_ready, DC * a + c + 1)
                half = shifted[:, c * HC * S:(c + 1) * HC * S].rearrange("p (h k) -> p h k", h=HC)
                nc.vector.tensor_tensor(half, sc, mx.unsqueeze(2).to_broadcast([T, HC, S]), ALU.subtract
                                        ).then_inc(shift_ready, 1)

            def transpose_half(a, c):
                dve.wait_ge(exp_ready, DC * a + c + 1)
                for b in range(B):
                    r = slice(b * S, (b + 1) * S)
                    last = nc.vector.transpose(probsT[r, c * HC:(c + 1) * HC, r],
                                               probs[r, c * HC * S:(c + 1) * HC * S])
                last.then_inc(probsT_ready, 1)

            def attention_tail(a, src, dst):
                dve.wait_ge(pv_ready, DC * (a + 1))
                o = bO[:, 0:NH * (HD + 1)].rearrange("p (h d) -> p h d", h=NH)
                nc.vector.reciprocal(inv_sum[:, a], o[:, :, HD]).then_inc(inv_ready, 1)
                dve.wait_ge(inv_ready, a + 1)
                nc.vector.tensor_tensor(heads_out[:, a].rearrange("p (h d) -> p h d", h=NH), o[:, :, 0:HD],
                                        inv_sum[:, a].unsqueeze(2).to_broadcast([T, NH, HD]), ALU.mult
                                        ).then_inc(heads_ready, 1)
                dve.wait_ge(y_psum, a + 1)
                nc.vector.tensor_tensor(dst, bY[:, 0:D], src, ALU.add).then_inc(x_ready, 1)
                dve.wait_ge(x_ready, a + 1)

            dve.wait_ge(ld["x"], 16)
            layer_norm(0, x_sb[:])
            dve.wait_ge(ld["small"], 16)
            dve.wait_ge(k_psum, 1)
            for c in range(DC):
                spread_keys(0, c)
            for a in range(2):
                if a == 1:
                    layer_norm(1, x1[:])
                    dve.wait_ge(k_psum, 2)
                    for c in range(DC):
                        spread_keys(1, c)
                softmax_half(a, 0)
                softmax_half(a, 1)
                if a == 0:
                    dve.wait_ge(zeroed, 1)
                transpose_half(a, 0)
                transpose_half(a, 1)
                attention_tail(a, (x_sb[:], x1[:])[a], (x1[:], x2[:])[a])
            layer_norm(2, x2[:])

            def step(ins):
                link(ins, "route", route_step)

            logits = bQ[:, 0:E]
            dve.wait_ge(e_abs_ready, 1)
            nc.vector.tensor_scalar(one_plus[:], e_abs[:], 1.0, None, ALU.add).then_inc(one_plus_ready, 1)
            dve.wait_ge(one_plus_ready, 1)
            step(nc.vector.tensor_scalar(den[:], one_plus[:], -1.0, TINY, ALU.add, ALU.add))
            step(nc.vector.reciprocal(den[:], den[:]))
            step(nc.vector.tensor_tensor(den[:], den[:], e_abs[:], ALU.mult))
            dve.wait_ge(ln_ready, 1)
            step(nc.vector.scalar_tensor_tensor(ratio[:], ln_one_plus[:], TINY, den[:], ALU.add, ALU.mult))
            nc.vector.scalar_tensor_tensor(softplus[:], logits, 0.0, ratio[:], ALU.max, ALU.add
                                           ).then_inc(softplus_ready, 1)
            dve.wait_ge(score_ready, 1)
            dve.wait_ge(zeroed, 3)
            step(nc.vector.tensor_tensor(key[:, 0:E], score[:], small_sb[:, EBIAS:EBIAS + E], ALU.add))
            step(nc.vector.max(top8[:], key[:, 0:E]))
            step(nc.vector.memset(top8[:, K:8], SENTINEL))
            step(nc.vector.match_replace(replaced[:], top8[:], key[:], -SENTINEL))
            step(nc.vector.tensor_tensor(chosen[:], replaced[:, 0:E], key[:, 0:E], ALU.not_equal))
            step(nc.vector.scalar_tensor_tensor(weight[:], chosen[:], 1.0, score[:], ALU.mult, ALU.mult,
                                                accum_out=weight_sum[:, 0:1]))
            step(nc.vector.tensor_scalar(weight_sum[:, 1:2], weight_sum[:, 0:1], 1e-20, None, ALU.add))
            step(nc.vector.reciprocal(weight_sum[:, 0:1], weight_sum[:, 1:2]))
            nc.vector.tensor_scalar(gate[:], weight[:], weight_sum[:, 0:1], None, ALU.mult).then_inc(gate_ready, 1)

            def clip(n, j, width=2):
                dve.wait_ge(gu_ready, n + 1)
                nc.vector.tensor_scalar(gu_clip[:, j, 0:width], bS[j][:, 0:width * 2 * I], CLIP, -CLIP,
                                        ALU.min, ALU.max).then_inc(clip_ready, 1)

            def unit(n, j):
                clip(n, j)
                dve.wait_ge(silu_ready, n + 1)
                dve.wait_ge(hT_psum, n - 1)
                for e in range(2):
                    last = nc.vector.scalar_tensor_tensor(h[:, j, e], gu_clip[:, j, e, 1, :],
                                                          gate[:, bass.ds((n - 1) * 2 + e, 1)], silu[:, j, e],
                                                          ALU.mult, ALU.mult)
                last.then_inc(h_ready, 1)

            clip(0, 0, width=1)
            dve.wait_ge(silu_ready, 1)
            nc.vector.tensor_tensor(h[:, 0, 0], gu_clip[:, 0, 0, 1, :], silu[:, 0, 0], ALU.mult).then_inc(h_ready, 1)
            dve.wait_ge(gate_ready, 1)
            clip(1, 1)
            dve.wait_ge(silu_ready, 2)
            for e in range(2):
                last = nc.vector.scalar_tensor_tensor(h[:, 1, e], gu_clip[:, 1, e, 1, :], gate[:, e:e + 1],
                                                      silu[:, 1, e], ALU.mult, ALU.mult)
            last.then_inc(h_ready, 1)
            with nc.vector.Fori(0, PAIRS // 2 - 1) as i:
                unit(i * 2 + 2, 0)
                unit(i * 2 + 3, 1)
            unit(PAIRS, 0)
            dve.wait_ge(y_done, PAIRS + 1)
            nc.vector.tensor_tensor(y_sb[:], bO[:, 0:D], x2[:], ALU.add).then_inc(fin, 1)


def kernel(**inputs):
    import ml_dtypes
    import numpy as np
    import concourse.bacc as bacc
    from concourse.bass_utils import run_bass_kernel_spmd

    v = {n: np.asarray(a) for n, a in inputs.items()}

    def chunked(w):
        return w.T.reshape(DC, 128, w.shape[0]).transpose(1, 0, 2)

    small = np.zeros((128, SMALL), np.float32)
    small[:, IDENT:IDENT + 128] = np.eye(128, dtype=np.float32)
    small[:, HMASK:HMASK + HC] = np.arange(128)[:, None] // HD == np.arange(HC)[None, :]
    small[:, BIASQ:BIASQ + DC] = v["L0_attn_bq"].reshape(DC, 128).T
    small[:, BIASK:BIASK + DC] = v["L0_attn_bk"].reshape(DC, 128).T
    small[:, EBIAS:EBIAS + E] = v["L0_ffn_expert_bias"][None, :]
    small[:, ROUTER:] = chunked(v["L0_ffn_router_w"]).reshape(128, DC * E)

    causal = np.zeros((128, 128 + HC * S), np.float32)
    causal[:, 0:128] = np.eye(128)
    hidden = np.arange(S)[None, :] > (np.arange(T) % S)[:, None]
    causal[:, 128:] = np.tile(np.where(hidden, -1e30, 0.0), (1, HC))
    causal = causal.astype(ml_dtypes.bfloat16)

    ctx_kv = np.concatenate([v["ctx_512"][:, :S].reshape(T, L).T, v["L0_xattn_Wkv_expand"].T], axis=1)
    lora = np.stack([np.stack([v["L0_attn_B" + m] for m in "qkvo"], axis=1),
                     np.stack([v["L0_attn_A" + m].T for m in "qkvo"], axis=1)], axis=1)
    rows = np.concatenate([np.ones(T, np.float32), v["L0_attn_bv"], v["L0_attn_bo"]])[None, :]
    attn_w = np.stack([chunked(v["L0_attn_W" + m]).reshape(128, DC * D) for m in "qkvo"], axis=1)

    shared_gu = np.concatenate([chunked(v["L0_ffn_shared_gate_w"]), chunked(v["L0_ffn_shared_up_w"])], axis=2)
    shared = np.concatenate([shared_gu.reshape(128, -1), v["L0_ffn_shared_down_w"].T], axis=1)
    gu = np.stack([v["L0_ffn_gate_w"], v["L0_ffn_up_w"]], axis=1)
    gu = gu.reshape(PAIRS, GU, DC, 128).transpose(3, 0, 2, 1).reshape(128, PAIRS, DC * GU)
    dn = v["L0_ffn_down_w"].transpose(2, 0, 1).reshape(128, PAIRS, 2 * D)
    moe = np.concatenate([gu, dn], axis=2).reshape(128, -1)

    arrays = {"x": v["x"].reshape(T, D), "small": small, "causal": causal, "ctx_kv": ctx_kv,
              "x_wq": chunked(v["L0_xattn_Wq"]), "x_wo": chunked(v["L0_xattn_Wout"]), "lora": lora, "rows": rows,
              "attn_w": attn_w, "shared_w": shared, "moe_w": moe}
    arrays = {n: np.ascontiguousarray(a) for n, a in arrays.items()}

    nc = bacc.Bacc("TRN2", target_bir_lowering=False, num_devices=1)
    args = {n: nc.dram_tensor(n + "_dram", a.shape, mybir.dt.from_np(a.dtype), kind="ExternalInput").ap()
            for n, a in arrays.items()}
    out = nc.dram_tensor("out_dram", (T, D), F32, kind="ExternalOutput").ap()
    build(nc, out=out, **args)
    r = run_bass_kernel_spmd(nc, [{n + "_dram": a for n, a in arrays.items()}], core_ids=[0])
    return r.results[0]["out_dram"].reshape(B, S, D)
```

```python
from contextlib import ExitStack

import concourse.bass as bass
from concourse import mybir

F32 = mybir.dt.float32
BF16 = mybir.dt.bfloat16
F32R = mybir.dt.float32r
ALU = mybir.AluOpType
ACT = mybir.ActivationFunctionType
AX_X = mybir.AxisListType.X

B, S, D, L = 4, 32, 256, 64
T = B * S
DC = D // 128
NH, HD = 16, 16
G = 4
NG = NH // G
V1 = HD + 1
R = 16
LORA_SCALE = 8.0 / R
SM_SCALE = HD ** -0.5
E, I, K = 32, 128, 4
CLIP = 7.0
WARM = (8, 0, 1, 1, 1, 1, 2, 1, 9, 1, 1, 0, 0, 0, 3, 1, 9, 1)
EPS = 1e-5
PAIRS = E // 2
GU = 4 * I
PAIR = DC * GU + 2 * D
RING = 4
RAW = 8
HI_LO = ((0, 0), (0, 1), (1, 0))
SENTINEL = 3e38
TINY = 1e-30

IDENT, HMASK, BIASQ, BIASK, BIASV, EBIAS, ROUTER = 0, 128, 132, 134, 136, 138, 170
SMALL = ROUTER + DC * E
CTX, WKV = 0, T
ONES, BO = 0, T


def build(nc, x, small, causal, ctx_kv, x_wq, x_wo, lora, rows, attn_w, shared_w, moe_w, out):
    with ExitStack() as ctx:
        def sb(name, shape, dt=F32):
            return ctx.enter_context(nc.sbuf_tensor(name, shape, dt))

        def pb(name):
            return ctx.enter_context(nc.psum_tensor(name, [128, 512], F32))

        def sem(name):
            return ctx.enter_context(nc.semaphore(name))

        x_sb = sb("x_sb", [T, D])
        small_sb = sb("small_sb", [128, SMALL])
        causal_sb = sb("causal_sb", [128, 128 + 2 * G * S], BF16)
        ctx_sb = sb("ctx_sb", [L, T + 2 * D])
        xwq_sb = sb("xwq_sb", [128, DC, D])
        xwo_sb = sb("xwo_sb", [128, DC, D])
        lora_sb = sb("lora_sb", [R, 2, 4, D])
        rows_sb = sb("rows_sb", [1, T + D])
        aw_sb = sb("aw_sb", [128, 4, DC * D])
        shared_sb = sb("shared_sb", [128, DC * 2 * I + D])
        gu_raw = sb("gu_raw", [128, RAW * DC * GU])
        gu_w = sb("gu_w", [128, RING, 2, DC * GU], F32R)
        dn_w = sb("dn_w", [128, PAIRS * 2 * D])

        ident = small_sb[:, IDENT:IDENT + 128]
        hmask = small_sb[:, HMASK:HMASK + G]

        stats = sb("stats", [T, 3, 6])
        moments = sb("moments", [T, 3, 2])
        var_eps = sb("var_eps", [T, 3])
        rstd = sb("rstd", [T, 3])
        inv_sqrt_power = sb("inv_sqrt_power", [T, 1])
        ln_floor = sb("ln_floor", [T, 1])
        xn = sb("xn", [T, 3, D])
        xnT = sb("xnT", [128, 3, DC, T])
        qT = sb("qT", [128, 2, DC, T])
        k_heads = sb("k_heads", [128, 2, DC, G, T])
        v_heads = sb("v_heads", [128, 2, B, NG, G, V1])
        row_max = sb("row_max", [T, 2, 2, NH // 2])
        shifted = sb("shifted", [T, 2, 2 * G * S])
        probs = sb("probs", [T, 2, 2 * G * S])
        probsT = sb("probsT", [128, 2, 2, T])
        inv_sum = sb("inv_sum", [T, 2, NH])
        heads_out = sb("heads_out", [T, 2, D])
        heads_outT = sb("heads_outT", [128, 2, DC, T])
        x1 = sb("x1", [T, D])
        warm_sb = sb("warm_sb", [128, 512], BF16)
        x2 = sb("x2", [T, D])
        abs_logits = sb("abs_logits", [T, E])
        e_abs = sb("e_abs", [T, E])
        one_plus = sb("one_plus", [T, E])
        ln_one_plus = sb("ln_one_plus", [T, E])
        den = sb("den", [T, E])
        ratio = sb("ratio", [T, E])
        softplus = sb("softplus", [T, E])
        ln_softplus = sb("ln_softplus", [T, E])
        half_power = sb("half_power", [T, E])
        root = sb("root", [T, E])
        inv_root = sb("inv_root", [T, E])
        score2 = sb("score2", [T, E])
        key = sb("key", [T, E + K])
        top8 = sb("top8", [T, 8])
        replaced = sb("replaced", [T, E + K])
        chosen = sb("chosen", [T, E])
        weight = sb("weight", [T, E])
        weight_sum = sb("weight_sum", [T, 2])
        gate = sb("gate", [T, E])
        gu_clip = sb("gu_clip", [T, 4, 2, 2, I])
        silu = sb("silu", [T, 2, 2, I])
        h = sb("h", [T, 2, 2, I])
        hT = sb("hT", [128, 2, 2, T])
        xnT_parts = sb("xnT_parts", [128, 2, DC, T], F32R)
        y_sb = sb("y_sb", [T, D])

        bK, bV, bT, bQ, bS0, bS1, bO, bY = (pb(n) for n in ("bK", "bV", "bT", "bQ", "bS0", "bS1", "bO", "bY"))
        bS = (bS0, bS1)
        bKK = (bK, bY)
        bH = (bK, bV)
        bGU = (bT, bS0, bS1, bY)

        ld = {n: sem("ld_" + n) for n in ("x", "small", "causal", "ctx", "xwq", "xwo", "lora", "rows",
                                          "aw", "shared")}
        ld_gu = [sem(f"ld_gu{j}") for j in range(2)]
        ld_dn = [sem(f"ld_dn{j}") for j in range(2)]
        zeroed = sem("zeroed")
        ln_step = sem("ln_step")
        warm_set = sem("warm_set")
        var_ready = sem("var_ready")
        rstd_ready = sem("rstd_ready")
        softplus_ready = sem("softplus_ready")
        ln_softplus_ready = sem("ln_softplus_ready")
        half_power_ready = sem("half_power_ready")
        root_ready = sem("root_ready")
        powers_set = sem("powers_set")
        xn_ready = sem("xn_ready")
        xnT_psum = sem("xnT_psum")
        xnT_ready = sem("xnT_ready")
        k_psum = sem("k_psum")
        v_psum = sem("v_psum")
        q_psum = sem("q_psum")
        k_ready = sem("k_ready")
        v_ready = sem("v_ready")
        q_ready = sem("q_ready")
        lora_psum = sem("lora_psum")
        lora_merged = sem("lora_merged")
        scores_ready = sem("scores_ready")
        max_ready = sem("max_ready")
        shift_ready = sem("shift_ready")
        exp_ready = sem("exp_ready")
        probsT_psum = sem("probsT_psum")
        probsT_ready = sem("probsT_ready")
        pv_ready = sem("pv_ready")
        inv_ready = sem("inv_ready")
        heads_ready = sem("heads_ready")
        headsT_psum = sem("headsT_psum")
        headsT_ready = sem("headsT_ready")
        y_psum = sem("y_psum")
        x_ready = sem("x_ready")
        logits_ready = sem("logits_ready")
        abs_ready = sem("abs_ready")
        e_abs_ready = sem("e_abs_ready")
        one_plus_ready = sem("one_plus_ready")
        ln_ready = sem("ln_ready")
        route_step = sem("route_step")
        gate_ready = sem("gate_ready")
        gu_ready = sem("gu_ready")
        clip_ready = sem("clip_ready")
        silu_ready = sem("silu_ready")
        h_ready = sem("h_ready")
        hT_psum = sem("hT_psum")
        hT_ready = sem("hT_ready")
        xnT_hi_ready = sem("xnT_hi_ready")
        xnT_parts_ready = sem("xnT_parts_ready")
        gu_hi_ready = sem("gu_hi_ready")
        gu_lo_ready = [sem(f"gu_lo_ready{c}") for c in range(DC)]
        y_done = sem("y_done")
        fin = sem("fin")
        stored = sem("stored")

        block = ctx.enter_context(nc.Block())

        @block.sync
        def _(sp):
            for name, dst, src in (("x", x_sb, x), ("small", small_sb, small), ("causal", causal_sb, causal),
                                   ("lora", lora_sb, lora), ("aw", aw_sb, attn_w), ("xwo", xwo_sb, x_wo),
                                   ("rows", rows_sb, rows), ("shared", shared_sb, shared_w)):
                sp.dma_start(dst[:], src).then_inc(ld[name], 16)

            def load_gu(p, slot, j, before):
                if before is not None:
                    sp.wait_ge(ld_gu[j], before * 16)
                nc.sync.dma_start(gu_raw[:, bass.ds(slot * (DC * GU), DC * GU)], moe_w[:, bass.ds(p * PAIR, DC * GU)]
                                  ).then_inc(ld_gu[j], 16)

            def load_dn(p, j, before):
                if before is not None:
                    sp.wait_ge(ld_dn[j], before * 16)
                nc.sync.dma_start(dn_w[:, bass.ds(p * (2 * D), 2 * D)], moe_w[:, bass.ds(p * PAIR + DC * GU, 2 * D)]
                                  ).then_inc(ld_dn[j], 16)

            for p in range(RAW):
                load_gu(p, p, p % 2, p // 2 or None)
            for p in range(2):
                load_dn(p, p, None)
            with nc.sync.Fori(1, RAW // 2) as i:
                for u in range(2):
                    load_dn(i * 2 + u, u, i)
            with nc.sync.Fori(0, (PAIRS - RAW) // 2) as i:
                for u in range(2):
                    for c in range(DC):
                        sp.wait_ge(gu_lo_ready[c], i * 2 + (u + 1))
                    load_gu(i * 2 + (RAW + u), i * 2 + u, u, i + RAW // 2)
                    load_dn(i * 2 + (RAW + u), u, i + RAW // 2)
            sp.wait_ge(fin, 1)
            sp.dma_start(out, y_sb[:]).then_inc(stored, 16)
            sp.wait_ge(stored, 16)

        @block.gpsimd
        def _(pool):
            nc.gpsimd.memset(inv_sqrt_power[:], -0.5).then_inc(powers_set, 1)
            nc.gpsimd.memset(ln_floor[:], 2.0 ** -64).then_inc(powers_set, 1)
            nc.gpsimd.memset(v_heads[:], 0.0).then_inc(zeroed, 1)
            nc.gpsimd.memset(key[:, E:E + K], SENTINEL).then_inc(zeroed, 1)
            pool.wait_ge(zeroed, 2)
            for j in range(G):
                nc.gpsimd.memset(v_heads[j * S:(j + 1) * S, :, :, :, j, HD], 1.0).then_inc(zeroed, 1)
            pool.wait_ge(zeroed, 2 + G)

            pool.wait_ge(powers_set, 2)

            def inverse_sqrt(n):
                pool.wait_ge(var_ready, n + 1)
                nc.gpsimd.tensor_tensor(rstd[:, n:n + 1], var_eps[:, n:n + 1], inv_sqrt_power[:], ALU.pow
                                        ).then_inc(rstd_ready, 1)

            inverse_sqrt(0)

            def gu_low(p, slot, raw, c):
                pool.wait_ge(gu_hi_ready, p + 1)
                nc.gpsimd.tensor_tensor(gu_w[:, slot, 1, c * GU:(c + 1) * GU],
                                        gu_raw[:, bass.ds(raw * (DC * GU) + c * GU, GU)],
                                        gu_w[:, slot, 0, c * GU:(c + 1) * GU], ALU.subtract
                                        ).then_inc(gu_lo_ready[c], 1)

            for p in range(RING):
                if p == 2:
                    inverse_sqrt(1)
                for c in range(DC):
                    gu_low(p, p, p, c)
            inverse_sqrt(2)
            for p in range(RING, RAW):
                gu_low(p, p % RING, p, 0)
            with nc.gpsimd.Fori(0, (PAIRS - RAW) // RING) as i:
                for u in range(RING):
                    gu_low(i * RING + (RAW + u), u, i * RING + u, 0)

        @block.tensor
        def _(pe):
            def merge_lora(m, bank):
                for c in range(DC):
                    last = nc.tensor.matmul(bank[:, c * D:(c + 1) * D], lora_sb[:, 0, m, c * 128:(c + 1) * 128],
                                            lora_sb[:, 1, m, :], start=True, stop=True)
                last.then_inc(lora_psum, 1)

            def transpose_xn(n):
                pe.wait_ge(xn_ready, n + 1)
                for c in range(DC):
                    last = nc.tensor.transpose(bT[:, c * T:(c + 1) * T], xn[:, n, c * 128:(c + 1) * 128], ident)
                last.then_inc(xnT_psum, 1)

            def project_T(banks, side, w, a, done):
                for c in range(DC):
                    for k in range(DC):
                        last = nc.tensor.matmul(banks[c][:, side * c * T:(side * c + 1) * T],
                                                w[:, k, c * 128:(c + 1) * 128], xnT[:, a, k, :],
                                                start=(k == 0), stop=(k == DC - 1))
                    if c == DC - 1 or not side:
                        last.then_inc(done, 1)

            def keep_warm(bank, n):
                for _ in range(n):
                    nc.tensor.matmul(bank[:, :], warm_sb[:, 0:128], warm_sb[:, :], start=True, stop=True)

            def values(a, x_t, w, chunks):
                for b in range(B):
                    for k in range(chunks):
                        for j in range(G):
                            last = nc.tensor.matmul(
                                bV[j * S:(j + 1) * S, b * NG * HD:(b + 1) * NG * HD],
                                x_t(k)[:, b * S:(b + 1) * S],
                                w(k).rearrange("p (n j d) -> p n j d", j=G, d=HD)[:, :, j, :],
                                start=(k == 0), stop=(k == chunks - 1), skip_group_check=True)
                last.then_inc(v_psum, 1)

            def scores(a, g):
                r = slice(64 * g, 64 * g + 64)
                if a == 0:
                    nc.tensor.matmul(bS[g][:, 0:2 * G * S], causal_sb[:, 0:128], causal_sb[:, 128:],
                                     start=True, stop=False, skip_group_check=True)
                for c in range(DC):
                    for b in range(B):
                        last = nc.tensor.matmul(bS[g][b * S:(b + 1) * S, c * G * S:(c + 1) * G * S],
                                                qT[r, a, c, b * S:(b + 1) * S],
                                                k_heads[r, a, c, :, b * S:(b + 1) * S],
                                                start=(a == 1), stop=True, skip_group_check=True)
                last.then_inc(scores_ready, 1)

            def transpose_probs(a, g):
                pe.wait_ge(exp_ready, 2 * a + g + 1)
                for c in range(DC):
                    last = nc.tensor.transpose((bT, bK)[g][:, c * T:(c + 1) * T],
                                               probs[:, g, c * G * S:(c + 1) * G * S], ident)
                last.then_inc(probsT_psum, 1)

            def attend(a, g):
                pe.wait_ge(probsT_ready, 2 * a + g + 1)
                for c in range(DC):
                    n = 2 * c + g
                    for b in range(B):
                        last = nc.tensor.matmul(bO[b * S:(b + 1) * S, n * G * V1:(n + 1) * G * V1],
                                                probsT[:, g, c, b * S:(b + 1) * S], v_heads[:, a, b, n],
                                                start=True, stop=True, skip_group_check=True)
                last.then_inc(pv_ready, 1)

            def project_out(a, w):
                pe.wait_ge(heads_ready, a + 1)
                for c in range(DC):
                    last = nc.tensor.transpose(bT[:, c * T:(c + 1) * T], heads_out[:, a, c * 128:(c + 1) * 128], ident)
                last.then_inc(headsT_psum, 1)
                keep_warm(bS0, WARM[7 + 8 * a])
                pe.wait_ge(headsT_ready, a + 1)
                for c in range(DC):
                    last = nc.tensor.matmul(bY[:, 0:D], heads_outT[:, a, c, :], w[:, c, :],
                                            start=(a == 0 and c == 0), stop=(c == DC - 1))
                last.then_inc(y_psum, 1)

            pe.wait_ge(warm_set, 1)
            keep_warm(bS0, WARM[0])
            pe.wait_ge(ld["ctx"], 16)
            for c in range(DC):
                nc.tensor.matmul(bKK[c][:, 0:T], ctx_sb[:, WKV + c * 128:WKV + (c + 1) * 128],
                                 ctx_sb[:, CTX:CTX + T], start=True, stop=True).then_inc(k_psum, 1)
            pe.wait_ge(ld["small"], 16)
            keep_warm(bS0, WARM[1])
            transpose_xn(0)
            values(0, lambda k: ctx_sb[:, CTX:CTX + T], lambda k: ctx_sb[:, WKV + D:WKV + 2 * D], 1)
            keep_warm(bS0, WARM[2])
            pe.wait_ge(ld["xwq"], 16)
            pe.wait_ge(xnT_ready, 1)
            project_T((bQ, bQ), 1, xwq_sb, 0, q_psum)
            keep_warm(bO, WARM[3])
            pe.wait_ge(ld["causal"], 16)
            pe.wait_ge(q_ready, 1)
            pe.wait_ge(k_ready, 2)
            scores(0, 0)
            scores(0, 1)
            pe.wait_ge(ld["lora"], 16)
            merge_lora(0, bY)
            keep_warm(bO, WARM[4])
            transpose_probs(0, 0)
            transpose_probs(0, 1)
            merge_lora(1, bQ)
            keep_warm(bS0, WARM[5])
            pe.wait_ge(v_ready, 2)
            attend(0, 0)
            attend(0, 1)
            merge_lora(2, bV)
            keep_warm(bS0, WARM[6])
            pe.wait_ge(ld["xwo"], 16)
            pe.wait_ge(lora_merged, 1)
            project_out(0, xwo_sb)
            merge_lora(3, bO)
            keep_warm(bS0, WARM[8])

            transpose_xn(1)
            keep_warm(bS0, WARM[9])
            pe.wait_ge(xnT_ready, 2)
            aw = [aw_sb[:, m].rearrange("p (c n) -> p c n", c=DC) for m in range(4)]
            pe.wait_ge(lora_merged, 1)
            project_T(bKK, 0, aw[0], 1, k_psum)
            pe.wait_ge(lora_merged, 2)
            project_T((bQ, bQ), 1, aw[1], 1, q_psum)
            keep_warm(bS1, WARM[10])
            pe.wait_ge(q_ready, 2)
            pe.wait_ge(k_ready, 4)
            scores(1, 0)
            scores(1, 1)
            pe.wait_ge(lora_merged, 3)
            values(1, lambda k: xnT[:, 1, k, :], lambda k: aw[2][:, k, :], DC)
            keep_warm(bO, WARM[12])
            transpose_probs(1, 0)
            pe.wait_ge(ld["rows"], 16)
            nc.tensor.matmul(bY[:, 0:D], rows_sb[:, ONES:ONES + T], rows_sb[:, BO:BO + D], start=True, stop=False)
            transpose_probs(1, 1)
            pe.wait_ge(lora_merged, 4)
            for c in range(DC):
                nc.tensor.matmul(bY[:, 0:D], small_sb[:, BIASV + c:BIASV + c + 1].to_broadcast([128, T]),
                                 aw[3][:, c, :], start=False, stop=False)
            keep_warm(bS0, WARM[13])
            pe.wait_ge(v_ready, 4)
            attend(1, 0)
            attend(1, 1)
            keep_warm(bS0, WARM[14])
            project_out(1, aw[3])
            keep_warm(bS0, WARM[16])

            transpose_xn(2)
            keep_warm(bS0, WARM[17])
            pe.wait_ge(xnT_ready, 3)
            for k in range(DC):
                last = nc.tensor.matmul(bQ[:, 0:E], xnT[:, 2, k, :], small_sb[:, ROUTER + k * E:ROUTER + (k + 1) * E],
                                        start=(k == 0), stop=(k == DC - 1))
            last.then_inc(logits_ready, 1)

            def gate_up(n, j):
                if not (isinstance(n, int) and n <= 3):
                    pe.wait_ge(clip_ready, n - 3)
                for k in range(DC):
                    pe.wait_ge(gu_lo_ready[k], n)
                    for a, w in HI_LO:
                        last = nc.tensor.matmul(bGU[j][:, 0:GU], xnT_parts[:, a, k, :],
                                                gu_w[:, (j - 1) % RING, w, k * GU:(k + 1) * GU],
                                                start=(k == 0 and a == w == 0), stop=(k == DC - 1 and a == 1))
                last.then_inc(gu_ready, 1)

            def transpose_h(n, j, width=2):
                pe.wait_ge(h_ready, n + 1)
                for e in range(width):
                    last = nc.tensor.transpose(bH[j % 2][:, e * T:(e + 1) * T], h[:, j % 2, e, :], ident)
                last.then_inc(hT_psum, 1)

            def down(n, j, visit, stop=False):
                pe.wait_ge(ld_dn[(j + 1) % 2], visit * 16)
                pe.wait_ge(hT_ready, n + 1)
                for e in range(2):
                    last = nc.tensor.matmul(bO[:, 0:D], hT[:, j % 2, e, :],
                                            dn_w[:, bass.ds((n - 1) * (2 * D) + e * D, D)],
                                            start=False, stop=(stop and e == 1), skip_group_check=True)
                last.then_inc(y_done, 1)

            pe.wait_ge(ld["shared"], 16)
            pe.wait_ge(xnT_parts_ready, 1)
            for k in range(DC):
                last = nc.tensor.matmul(bGU[0][:, 0:2 * I], xnT[:, 2, k, :], shared_sb[:, k * 2 * I:(k + 1) * 2 * I],
                                        start=(k == 0), stop=(k == DC - 1))
            last.then_inc(gu_ready, 1)
            for n in range(1, 6):
                gate_up(n, n % 4)
            transpose_h(0, 0, width=1)
            transpose_h(1, 1)
            gate_up(6, 2)
            pe.wait_ge(hT_ready, 1)
            nc.tensor.matmul(bO[:, 0:D], hT[:, 0, 0, :], shared_sb[:, DC * 2 * I:], start=True, stop=False,
                             skip_group_check=True).then_inc(y_done, 1)
            transpose_h(2, 2)
            down(1, 1, 1)
            with nc.tensor.Fori(0, (PAIRS - RAW) // 4) as i:
                for u in range(3, 7):
                    gate_up(i * 4 + (u + 4), u % 4)
                    transpose_h(i * 4 + u, u % 4)
                    down(i * 4 + (u - 1), (u - 1) % 4, i * 2 + u // 2)
            for n in range(PAIRS - 5, PAIRS + 1):
                if n + 4 <= PAIRS:
                    gate_up(n + 4, n % 4)
                transpose_h(n, n % 4)
                down(n - 1, (n - 1) % 4, n // 2)
            down(PAIRS, 0, PAIRS // 2, stop=True)

        @block.scalar
        def _(act):
            act.dma_start(ctx_sb[:], ctx_kv).then_inc(ld["ctx"], 16)
            act.dma_start(xwq_sb[:], x_wq).then_inc(ld["xwq"], 16)
            nc.scalar.preload_act_table_set("natural_log_exp_and_others")

            def exp_half(a, g):
                act.wait_ge(shift_ready, 2 * a + g + 1)
                nc.scalar.activation(probs[:, g], shifted[:, g], ACT.Exp, scale=SM_SCALE).then_inc(exp_ready, 1)

            def copy_xnT(n):
                act.wait_ge(xnT_psum, n + 1)
                nc.scalar.activation(xnT[:, n], bT[:, 0:DC * T], ACT.Copy).then_inc(xnT_ready, 1)

            def copy_v(a, heads):
                act.wait_ge(v_psum, a + 1)
                for j in heads:
                    r = slice(j * S, (j + 1) * S)
                    last = nc.scalar.activation(v_heads[r, a, :, :, j, 0:HD],
                                                bV[r, 0:D].rearrange("p (b n d) -> p b n d", b=B, d=HD), ACT.Copy)
                return last

            def gu_high(p, slot, raw, visit):
                act.wait_ge(ld_gu[slot % 2], visit * 16)
                if not (isinstance(p, int) and p < RING):
                    act.wait_ge(gu_ready, p - 2)
                nc.scalar.activation(gu_w[:, slot, 0], gu_raw[:, bass.ds(raw * (DC * GU), DC * GU)], ACT.Copy
                                     ).then_inc(gu_hi_ready, 1)

            def copy_headsT(a):
                act.wait_ge(headsT_psum, a + 1)
                nc.scalar.activation(heads_outT[:, a], bT[:, 0:DC * T], ACT.Copy).then_inc(headsT_ready, 1)

            act.wait_ge(zeroed, 2 + G)
            copy_xnT(0)
            copy_v(0, (0,))
            act.wait_ge(q_psum, 1)
            nc.scalar.activation(qT[:, 0], bQ[:, 0:DC * T], ACT.Copy).then_inc(q_ready, 1)
            copy_v(0, (1, 2)).then_inc(v_ready, 1)
            exp_half(0, 0)
            exp_half(0, 1)
            for p in range(2):
                gu_high(p, p, p, 1)
            copy_headsT(0)
            for p in range(2, RING):
                gu_high(p, p, p, 2)

            copy_xnT(1)
            act.wait_ge(q_psum, 2)
            for c in range(DC):
                last = nc.scalar.activation(qT[:, 1, c], bQ[:, c * T:(c + 1) * T], ACT.Identity,
                                            bias=small_sb[:, BIASQ + c:BIASQ + c + 1])
            last.then_inc(q_ready, 1)
            exp_half(1, 0)
            copy_v(1, (0,))
            exp_half(1, 1)
            copy_v(1, (1, 2)).then_inc(v_ready, 1)
            copy_headsT(1)

            copy_xnT(2)
            nc.scalar.activation(xnT_parts[:, 0], bT[:, 0:DC * T], ACT.Copy).then_inc(xnT_hi_ready, 1)
            act.wait_ge(logits_ready, 1)
            nc.scalar.activation(abs_logits[:], bQ[:, 0:E], ACT.Abs).then_inc(abs_ready, 1)
            act.wait_ge(abs_ready, 1)
            nc.scalar.activation(e_abs[:], abs_logits[:], ACT.Exp, scale=-1.0).then_inc(e_abs_ready, 1)
            act.wait_ge(one_plus_ready, 1)
            nc.scalar.activation(ln_one_plus[:], one_plus[:], ACT.Ln).then_inc(ln_ready, 1)
            act.wait_ge(softplus_ready, 1)
            act.wait_ge(powers_set, 2)
            nc.scalar.activation(ln_softplus[:], softplus[:], ACT.Ln, bias=ln_floor[:]
                                 ).then_inc(ln_softplus_ready, 1)
            act.wait_ge(half_power_ready, 1)
            nc.scalar.activation(root[:], half_power[:], ACT.Exp, scale=0.5).then_inc(root_ready, 1)
            nc.scalar.preload_act_table(ACT.Silu)

            def silu_unit(n, j, width=2):
                act.wait_ge(clip_ready, n + 1)
                nc.scalar.activation(silu[:, j % 2, 0:width], gu_clip[:, j, 0:width, 0, :], ACT.Silu
                                     ).then_inc(silu_ready, 1)

            def hT_unit(n, j, width=2):
                act.wait_ge(hT_psum, n + 1)
                nc.scalar.activation(hT[:, j, 0:width], bH[j][:, 0:width * T], ACT.Copy).then_inc(hT_ready, 1)

            silu_unit(0, 0, width=1)
            gu_high(4, 0, 4, 3)
            silu_unit(1, 1)
            gu_high(5, 1, 5, 3)
            hT_unit(0, 0, width=1)
            for n in (1, 2):
                silu_unit(n + 1, (n + 1) % 4)
                gu_high(n + 5, (n + 5) % RING, n + 5, (n + 5) // 2 + 1)
                hT_unit(n, n % 2)
            with nc.scalar.Fori(0, (PAIRS - RAW) // RING) as i:
                for u in range(RING):
                    silu_unit(i * RING + (4 + u), u)
                    gu_high(i * RING + (RAW + u), u, i * RING + u, i * (RING // 2) + (RAW + u) // 2 + 1)
                    hT_unit(i * RING + (3 + u), (3 + u) % 2)
            for n in range(PAIRS - 5, PAIRS):
                silu_unit(n + 1, (n + 1) % 4)
                hT_unit(n, n % 2)
            hT_unit(PAIRS, 0)

        @block.vector
        def _(dve):
            links = {"ln": 0, "route": 0}

            def link(ins, which, s):
                links[which] += 1
                ins.then_inc(s, 1)
                dve.wait_ge(s, links[which])

            def layer_norm(n, src):
                link(nc.vector.bn_stats(stats[:, n], src), "ln", ln_step)
                link(nc.vector.bn_aggr(moments[:, n], stats[:, n]), "ln", ln_step)
                nc.vector.tensor_scalar(var_eps[:, n:n + 1], moments[:, n, 1:2], EPS, None, ALU.add
                                        ).then_inc(var_ready, 1)
                if n == 0:
                    dve.wait_ge(ld["small"], 16)
                dve.wait_ge(rstd_ready, n + 1)
                nc.vector.tensor_scalar(xn[:, n], src, moments[:, n, 0:1], rstd[:, n:n + 1],
                                        ALU.subtract, ALU.mult).then_inc(xn_ready, 1)

            def spread_keys(a, c):
                dve.wait_ge(k_psum, DC * a + c + 1)
                src = bKK[c][:, 0:T].unsqueeze(1).to_broadcast([128, G, T])
                mask = hmask.unsqueeze(2).to_broadcast([128, G, T])
                if a == 0:
                    ins = nc.vector.tensor_tensor(k_heads[:, a, c], src, mask, ALU.mult)
                else:
                    ins = nc.vector.scalar_tensor_tensor(k_heads[:, a, c], src, small_sb[:, BIASK + c:BIASK + c + 1],
                                                         mask, ALU.add, ALU.mult)
                ins.then_inc(k_ready, 1)

            def shift_half(a, g):
                dve.wait_ge(scores_ready, 2 * a + g + 1)
                sc = bS[g][:, 0:2 * G * S].rearrange("p (h k) -> p h k", k=S)
                nc.vector.tensor_reduce(row_max[:, a, g], sc, AX_X, ALU.max).then_inc(max_ready, 1)
                dve.wait_ge(max_ready, 2 * a + g + 1)
                nc.vector.tensor_tensor(shifted[:, g].rearrange("p (h k) -> p h k", k=S), sc,
                                        row_max[:, a, g].unsqueeze(2).to_broadcast([T, 2 * G, S]), ALU.subtract
                                        ).then_inc(shift_ready, 1)

            def copy_probsT(a, g):
                dve.wait_ge(probsT_psum, 2 * a + g + 1)
                nc.vector.tensor_copy(probsT[:, g], (bT, bK)[g][:, 0:DC * T]).then_inc(probsT_ready, 1)

            def copy_v(a):
                dve.wait_ge(v_psum, a + 1)
                dve.wait_ge(zeroed, 2 + G)
                j = G - 1
                r = slice(j * S, (j + 1) * S)
                nc.vector.tensor_copy(v_heads[r, a, :, :, j, 0:HD],
                                      bV[r, 0:D].rearrange("p (b n d) -> p b n d", b=B, d=HD)).then_inc(v_ready, 1)

            def merge_lora(m, bank):
                dve.wait_ge(lora_psum, m + 1)
                nc.vector.scalar_tensor_tensor(aw_sb[:, m], bank[:, :], LORA_SCALE, aw_sb[:, m],
                                               ALU.mult, ALU.add).then_inc(lora_merged, 1)

            def attention_tail(a, src, dst):
                dve.wait_ge(pv_ready, 2 * (a + 1))
                o = bO[:, 0:NH * V1].rearrange("p (h d) -> p h d", h=NH)
                nc.vector.reciprocal(inv_sum[:, a], o[:, :, HD]).then_inc(inv_ready, 1)
                dve.wait_ge(inv_ready, a + 1)
                nc.vector.tensor_tensor(heads_out[:, a].rearrange("p (h d) -> p h d", h=NH), o[:, :, 0:HD],
                                        inv_sum[:, a].unsqueeze(2).to_broadcast([T, NH, HD]), ALU.mult
                                        ).then_inc(heads_ready, 1)
                if a == 0:
                    merge_lora(1, bQ)
                    merge_lora(2, bV)
                dve.wait_ge(y_psum, a + 1)
                nc.vector.tensor_tensor(dst, bY[:, 0:D], src, ALU.add).then_inc(x_ready, 1)
                dve.wait_ge(x_ready, a + 1)

            nc.vector.memset(warm_sb[:], 1.0).then_inc(warm_set, 1)
            dve.wait_ge(ld["x"], 16)
            layer_norm(0, x_sb[:])
            for c in range(DC):
                spread_keys(0, c)
            for a in range(2):
                if a == 1:
                    layer_norm(1, x1[:])
                    merge_lora(3, bO)
                    for c in range(DC):
                        spread_keys(1, c)
                shift_half(a, 0)
                shift_half(a, 1)
                copy_v(a)
                copy_probsT(a, 0)
                copy_probsT(a, 1)
                if a == 0:
                    dve.wait_ge(ld["aw"], 16)
                    merge_lora(0, bY)
                attention_tail(a, (x_sb[:], x1[:])[a], (x1[:], x2[:])[a])
            layer_norm(2, x2[:])
            dve.wait_ge(xnT_hi_ready, 1)
            nc.vector.tensor_tensor(xnT_parts[:, 1], bT[:, 0:DC * T], xnT_parts[:, 0], ALU.subtract
                                    ).then_inc(xnT_parts_ready, 1)

            def clip(n, j, width=2):
                dve.wait_ge(gu_ready, n + 1)
                if not (isinstance(n, int) and n < 4):
                    dve.wait_ge(h_ready, n - 3)
                nc.vector.tensor_scalar(gu_clip[:, j, 0:width], bGU[j][:, 0:width * 2 * I], CLIP, -CLIP,
                                        ALU.min, ALU.max).then_inc(clip_ready, 1)

            def step(ins):
                link(ins, "route", route_step)

            logits = bQ[:, 0:E]
            dve.wait_ge(e_abs_ready, 1)
            nc.vector.tensor_scalar(one_plus[:], e_abs[:], 1.0, None, ALU.add).then_inc(one_plus_ready, 1)
            dve.wait_ge(one_plus_ready, 1)
            step(nc.vector.tensor_scalar(den[:], one_plus[:], -1.0, TINY, ALU.add, ALU.add))
            step(nc.vector.reciprocal(den[:], den[:]))
            step(nc.vector.tensor_tensor(den[:], den[:], e_abs[:], ALU.mult))
            dve.wait_ge(ln_ready, 1)
            step(nc.vector.scalar_tensor_tensor(ratio[:], ln_one_plus[:], TINY, den[:], ALU.add, ALU.mult))
            nc.vector.scalar_tensor_tensor(softplus[:], logits, 0.0, ratio[:], ALU.max, ALU.add
                                           ).then_inc(softplus_ready, 1)
            dve.wait_ge(ln_softplus_ready, 1)
            nc.vector.scalar_tensor_tensor(half_power[:], logits, -100.0, ln_softplus[:], ALU.max, ALU.min
                                           ).then_inc(half_power_ready, 1)
            clip(0, 0, width=1)
            dve.wait_ge(root_ready, 1)
            step(nc.vector.reciprocal(inv_root[:], root[:]))
            step(nc.vector.tensor_tensor(inv_root[:], inv_root[:], softplus[:], ALU.mult))
            step(nc.vector.tensor_tensor(score2[:], inv_root[:], root[:], ALU.add))
            dve.wait_ge(zeroed, 2)
            step(nc.vector.scalar_tensor_tensor(key[:, 0:E], score2[:], 0.5, small_sb[:, EBIAS:EBIAS + E],
                                                ALU.mult, ALU.add))
            clip(1, 1)
            step(nc.vector.max(top8[:], key[:, 0:E]))
            step(nc.vector.memset(top8[:, K:8], SENTINEL))
            step(nc.vector.match_replace(replaced[:], top8[:], key[:], -SENTINEL))
            step(nc.vector.tensor_tensor(chosen[:], replaced[:, 0:E], key[:, 0:E], ALU.not_equal))
            step(nc.vector.scalar_tensor_tensor(weight[:], chosen[:], 0.5, score2[:], ALU.mult, ALU.mult,
                                                accum_out=weight_sum[:, 0:1]))
            step(nc.vector.tensor_scalar(weight_sum[:, 1:2], weight_sum[:, 0:1], 1e-20, None, ALU.add))
            step(nc.vector.reciprocal(weight_sum[:, 0:1], weight_sum[:, 1:2]))
            nc.vector.tensor_scalar(gate[:], weight[:], weight_sum[:, 0:1], None, ALU.mult).then_inc(gate_ready, 1)

            def gu_low(p, slot, raw):
                dve.wait_ge(gu_hi_ready, p + 1)
                nc.vector.tensor_tensor(gu_w[:, slot, 1, GU:], gu_raw[:, bass.ds(raw * (DC * GU) + GU, GU)],
                                        gu_w[:, slot, 0, GU:], ALU.subtract).then_inc(gu_lo_ready[1], 1)

            def gate_h(n, j):
                dve.wait_ge(silu_ready, n + 1)
                if not (isinstance(n, int) and n < 2):
                    dve.wait_ge(hT_psum, n - 1)
                for e in range(2):
                    last = nc.vector.scalar_tensor_tensor(h[:, j % 2, e], gu_clip[:, j, e, 1, :],
                                                          gate[:, bass.ds((n - 1) * 2 + e, 1)], silu[:, j % 2, e],
                                                          ALU.mult, ALU.mult)
                last.then_inc(h_ready, 1)

            dve.wait_ge(silu_ready, 1)
            nc.vector.tensor_tensor(h[:, 0, 0], gu_clip[:, 0, 0, 1, :], silu[:, 0, 0], ALU.mult).then_inc(h_ready, 1)
            dve.wait_ge(gate_ready, 1)
            gu_low(4, 0, 4)
            for n in range(1, 4):
                clip(n + 1, (n + 1) % 4)
                gu_low(n + 4, n % RING, n + 4)
                gate_h(n, n % 4)
            with nc.vector.Fori(0, (PAIRS - RAW) // RING) as i:
                for u in range(RING):
                    clip(i * RING + (5 + u), (5 + u) % 4)
                    gu_low(i * RING + (RAW + u), u, i * RING + u)
                    gate_h(i * RING + (4 + u), u)
            for n in range(PAIRS - 4, PAIRS):
                clip(n + 1, (n + 1) % 4)
                gate_h(n, n % 4)
            gate_h(PAIRS, 0)
            dve.wait_ge(y_done, PAIRS + 1)
            nc.vector.tensor_tensor(y_sb[:], bO[:, 0:D], x2[:], ALU.add).then_inc(fin, 1)


def kernel(**inputs):
    import ml_dtypes
    import numpy as np
    import concourse.bacc as bacc
    from concourse.bass_utils import run_bass_kernel_spmd

    v = {n: np.asarray(a) for n, a in inputs.items()}

    def chunked(w):
        return w.T.reshape(DC, 128, w.shape[0]).transpose(1, 0, 2)

    small = np.zeros((128, SMALL), np.float32)
    small[:, IDENT:IDENT + 128] = np.eye(128, dtype=np.float32)
    small[:, HMASK:HMASK + G] = np.arange(128)[:, None] // HD % G == np.arange(G)[None, :]
    small[:, BIASV:BIASV + DC] = v["L0_attn_bv"].reshape(DC, 128).T
    small[:, BIASQ:BIASQ + DC] = v["L0_attn_bq"].reshape(DC, 128).T
    small[:, BIASK:BIASK + DC] = v["L0_attn_bk"].reshape(DC, 128).T
    small[:, EBIAS:EBIAS + E] = v["L0_ffn_expert_bias"][None, :]
    small[:, ROUTER:] = chunked(v["L0_ffn_router_w"]).reshape(128, DC * E)

    causal = np.zeros((128, 128 + 2 * G * S), np.float32)
    causal[:, 0:128] = np.eye(128)
    hidden = np.arange(S)[None, :] > (np.arange(T) % S)[:, None]
    causal[:, 128:] = np.tile(np.where(hidden, -1e30, 0.0), (1, 2 * G))
    causal = causal.astype(ml_dtypes.bfloat16)

    ctx_kv = np.concatenate([v["ctx_512"][:, :S].reshape(T, L).T, v["L0_xattn_Wkv_expand"].T], axis=1)
    lora = np.stack([np.stack([v["L0_attn_B" + m] for m in "kqvo"], axis=1),
                     np.stack([v["L0_attn_A" + m].T for m in "kqvo"], axis=1)], axis=1)
    rows = np.concatenate([np.ones(T, np.float32), v["L0_attn_bo"]])[None, :]
    attn_w = np.stack([chunked(v["L0_attn_W" + m]).reshape(128, DC * D) for m in "kqvo"], axis=1)

    shared_gu = np.concatenate([chunked(v["L0_ffn_shared_gate_w"]), chunked(v["L0_ffn_shared_up_w"])], axis=2)
    shared = np.concatenate([shared_gu.reshape(128, -1), v["L0_ffn_shared_down_w"].T], axis=1)
    gu = np.stack([v["L0_ffn_gate_w"], v["L0_ffn_up_w"]], axis=1)
    gu = gu.reshape(PAIRS, GU, DC, 128).transpose(3, 0, 2, 1).reshape(128, PAIRS, DC * GU)
    dn = v["L0_ffn_down_w"].transpose(2, 0, 1).reshape(128, PAIRS, 2 * D)
    moe = np.concatenate([gu, dn], axis=2).reshape(128, -1)

    arrays = {"x": v["x"].reshape(T, D), "small": small, "causal": causal, "ctx_kv": ctx_kv,
              "x_wq": chunked(v["L0_xattn_Wq"]), "x_wo": chunked(v["L0_xattn_Wout"]), "lora": lora, "rows": rows,
              "attn_w": attn_w, "shared_w": shared, "moe_w": moe}
    arrays = {n: np.ascontiguousarray(a) for n, a in arrays.items()}

    nc = bacc.Bacc("TRN2", target_bir_lowering=False, num_devices=1)
    args = {n: nc.dram_tensor(n + "_dram", a.shape, mybir.dt.from_np(a.dtype), kind="ExternalInput").ap()
            for n, a in arrays.items()}
    out = nc.dram_tensor("out_dram", (T, D), F32, kind="ExternalOutput").ap()
    build(nc, out=out, **args)
    r = run_bass_kernel_spmd(nc, [{n + "_dram": a for n, a in arrays.items()}], core_ids=[0])
    return r.results[0]["out_dram"].reshape(B, S, D)
```

```python
from contextlib import ExitStack

import concourse.bass as bass
from concourse import mybir

F32 = mybir.dt.float32
BF16 = mybir.dt.bfloat16
F32R = mybir.dt.float32r
ALU = mybir.AluOpType
ACT = mybir.ActivationFunctionType
AX_X = mybir.AxisListType.X

B, S, D, L = 4, 32, 256, 64
T = B * S
DC = D // 128
NH, HD = 16, 16
G = 4
NG = NH // G
V1 = HD + 1
R = 16
LORA_SCALE = 8.0 / R
SM_SCALE = HD ** -0.5
E, I, K = 32, 128, 4
CLIP = 7.0
WARM = (9, 1, 0, 0, 0, 0, 2, 1, 0, 0, 8, 1, 0, 1)
EPS = 1e-5
PAIRS = E // 2
GU = 4 * I
PAIR = DC * GU + 2 * D
RING = 4
RAW = 8
HI_LO = ((0, 0), (0, 1), (1, 0))
SENTINEL = 3e38
TINY = 1e-30

IDENT, HMASK, BIASQ, BIASK, BIASV, EBIAS, ROUTER = 0, 128, 132, 134, 136, 138, 170
SMALL = ROUTER + DC * E
CTX, WKV = 0, T
ONES, BO = 0, T


def build(nc, x, small, causal, ctx_kv, x_wq, x_wo, lora, rows, attn_w, shared_w, moe_w, out):
    with ExitStack() as ctx:
        def sb(name, shape, dt=F32):
            return ctx.enter_context(nc.sbuf_tensor(name, shape, dt))

        def pb(name):
            return ctx.enter_context(nc.psum_tensor(name, [128, 512], F32))

        def sem(name):
            return ctx.enter_context(nc.semaphore(name))

        x_sb = sb("x_sb", [T, D])
        small_sb = sb("small_sb", [128, SMALL])
        causal_sb = sb("causal_sb", [128, 128 + 2 * G * S], BF16)
        ctx_sb = sb("ctx_sb", [L, T + 2 * D])
        xwq_sb = sb("xwq_sb", [128, DC, D])
        xwo_sb = sb("xwo_sb", [128, DC, D])
        lora_sb = sb("lora_sb", [R, 2, 4, D])
        rows_sb = sb("rows_sb", [1, T + D])
        aw_sb = sb("aw_sb", [128, 4, DC * D])
        shared_sb = sb("shared_sb", [128, DC * 2 * I + D])
        gu_raw = sb("gu_raw", [128, (RAW + 1) * DC * GU])
        gu_w = sb("gu_w", [128, RING + 1, 2, DC * GU], F32R)
        dn_w = sb("dn_w", [128, PAIRS * 2 * D])

        ident = small_sb[:, IDENT:IDENT + 128]
        hmask = small_sb[:, HMASK:HMASK + G]

        stats = sb("stats", [T, 3, 6])
        moments = sb("moments", [T, 3, 2])
        var_eps = sb("var_eps", [T, 3])
        rstd = sb("rstd", [T, 3])
        inv_sqrt_power = sb("inv_sqrt_power", [T, 1])
        ln_floor = sb("ln_floor", [T, 1])
        xn = sb("xn", [T, 3, D])
        xnT = sb("xnT", [128, 3, DC, T])
        qT = sb("qT", [128, 2, DC, T])
        k_heads = sb("k_heads", [128, DC, G, T])
        v_heads = sb("v_heads", [128, B, NG, G, V1])
        row_max = sb("row_max", [T, 2, 2, NH // 2])
        shifted = sb("shifted", [T, 2, 2 * G * S])
        probs = sb("probs", [T, 2, 2 * G * S])
        probsT = sb("probsT", [128, 2, 2, T])
        inv_sum = sb("inv_sum", [T, 2, NH])
        heads_out = sb("heads_out", [T, 2, D])
        heads_outT = sb("heads_outT", [128, 2, DC, T])
        x1 = sb("x1", [T, D])
        warm_sb = sb("warm_sb", [128, 512], BF16)
        x2 = sb("x2", [T, D])
        abs_logits = sb("abs_logits", [T, E])
        e_abs = sb("e_abs", [T, E])
        one_plus = sb("one_plus", [T, E])
        ln_one_plus = sb("ln_one_plus", [T, E])
        den = sb("den", [T, E])
        ratio = sb("ratio", [T, E])
        softplus = sb("softplus", [T, E])
        ln_softplus = sb("ln_softplus", [T, E])
        half_power = sb("half_power", [T, E])
        root = sb("root", [T, E])
        inv_root = sb("inv_root", [T, E])
        score2 = sb("score2", [T, E])
        key = sb("key", [T, E + K])
        top8 = sb("top8", [T, 8])
        replaced = sb("replaced", [T, E + K])
        chosen = sb("chosen", [T, E])
        weight = sb("weight", [T, E])
        weight_sum = sb("weight_sum", [T, 2])
        gate = sb("gate", [T, E])
        gu_clip = sb("gu_clip", [T, 4, 2, 2, I])
        silu = sb("silu", [T, 2, 2, I])
        h = sb("h", [T, 2, 2, I])
        hT = sb("hT", [128, 2, 2, T])
        xnT_parts = sb("xnT_parts", [128, 2, DC, T], F32R)
        y_sb = sb("y_sb", [T, D])

        bK, bV, bT, bQ, bS0, bS1, bO, bY = (pb(n) for n in ("bK", "bV", "bT", "bQ", "bS0", "bS1", "bO", "bY"))
        bS = (bS0, bS1)
        bKK = (bK, bY)
        bH = (bK, bV)
        bXT = ((bT, bV), (bT, bV), (bT, bO))
        bHT = (bT, bK)
        bGU = (bT, bS0, bS1, bY)

        ld = {n: sem("ld_" + n) for n in ("x", "small", "causal", "ctx", "xwq", "xwo", "lora", "rows",
                                          "aw", "shared")}
        ld_gu = [sem(f"ld_gu{j}") for j in range(2)]
        ld_dn = [sem(f"ld_dn{j}") for j in range(2)]
        zeroed = sem("zeroed")
        ln_step = sem("ln_step")
        warm_set = sem("warm_set")
        var_ready = sem("var_ready")
        rstd_ready = sem("rstd_ready")
        softplus_ready = sem("softplus_ready")
        ln_softplus_ready = sem("ln_softplus_ready")
        half_power_ready = sem("half_power_ready")
        root_ready = sem("root_ready")
        powers_set = sem("powers_set")
        xn_ready = sem("xn_ready")
        xnT_psum = sem("xnT_psum")
        xnT_ready = sem("xnT_ready")
        k_psum = sem("k_psum")
        v_psum = sem("v_psum")
        q_psum = sem("q_psum")
        k_ready = sem("k_ready")
        v_ready = sem("v_ready")
        q_ready = sem("q_ready")
        lora_psum = sem("lora_psum")
        lora_merged = sem("lora_merged")
        scores_ready = sem("scores_ready")
        max_ready = sem("max_ready")
        shift_ready = sem("shift_ready")
        exp_ready = sem("exp_ready")
        probsT_psum = sem("probsT_psum")
        probsT_ready = sem("probsT_ready")
        pv_ready = sem("pv_ready")
        inv_ready = sem("inv_ready")
        heads_ready = sem("heads_ready")
        headsT_psum = sem("headsT_psum")
        headsT_ready = sem("headsT_ready")
        y_psum = sem("y_psum")
        x_ready = sem("x_ready")
        logits_ready = sem("logits_ready")
        abs_ready = sem("abs_ready")
        e_abs_ready = sem("e_abs_ready")
        one_plus_ready = sem("one_plus_ready")
        ln_ready = sem("ln_ready")
        route_step = sem("route_step")
        gate_ready = sem("gate_ready")
        gu_ready = sem("gu_ready")
        clip_ready = sem("clip_ready")
        silu_ready = sem("silu_ready")
        h_ready = sem("h_ready")
        hT_psum = sem("hT_psum")
        hT_ready = sem("hT_ready")
        xnT_hi_ready = sem("xnT_hi_ready")
        xnT_parts_ready = sem("xnT_parts_ready")
        gu_hi_ready = sem("gu_hi_ready")
        gu_lo_ready = [sem(f"gu_lo_ready{c}") for c in range(DC)]
        y_done = sem("y_done")
        fin = sem("fin")
        stored = sem("stored")

        block = ctx.enter_context(nc.Block())

        @block.sync
        def _(sp):
            for name, dst, src in (("x", x_sb, x), ("small", small_sb, small), ("causal", causal_sb, causal),
                                   ("lora", lora_sb, lora), ("aw", aw_sb, attn_w), ("xwo", xwo_sb, x_wo),
                                   ("rows", rows_sb, rows), ("shared", shared_sb, shared_w)):
                sp.dma_start(dst[:], src).then_inc(ld[name], 16)

            def load_gu(p, slot, j, before):
                if before is not None:
                    sp.wait_ge(ld_gu[j], before * 16)
                nc.sync.dma_start(gu_raw[:, bass.ds(slot * (DC * GU), DC * GU)], moe_w[:, bass.ds(p * PAIR, DC * GU)]
                                  ).then_inc(ld_gu[j], 16)

            def load_dn(p, j, before):
                if before is not None:
                    sp.wait_ge(ld_dn[j], before * 16)
                nc.sync.dma_start(dn_w[:, bass.ds(p * (2 * D), 2 * D)], moe_w[:, bass.ds(p * PAIR + DC * GU, 2 * D)]
                                  ).then_inc(ld_dn[j], 16)

            for p in range(RAW + 1):
                load_gu(p, p % RAW if p else RAW, p % 2, p // 2 or None)
            for p in range(RING):
                load_dn(p, p % 2, p // 2 or None)

            def reload(pairs):
                for p in pairs:
                    for c in range(DC):
                        sp.wait_ge(gu_lo_ready[c], p - RAW + 1)
                    load_gu(p, p - RAW, p % 2, p // 2)

            reload(range(RAW + 1, RAW + 1 + RING))
            with nc.sync.Fori(RING // 2, PAIRS // 2) as i:
                for u in range(2):
                    load_dn(i * 2 + u, u, i)
            reload(range(RAW + 1 + RING, PAIRS))
            sp.wait_ge(fin, 1)
            sp.dma_start(out, y_sb[:]).then_inc(stored, 16)
            sp.wait_ge(stored, 16)

        @block.gpsimd
        def _(pool):
            nc.gpsimd.memset(inv_sqrt_power[:], -0.5).then_inc(powers_set, 1)
            nc.gpsimd.memset(ln_floor[:], 2.0 ** -64).then_inc(powers_set, 1)
            nc.gpsimd.memset(v_heads[:], 0.0).then_inc(zeroed, 1)
            nc.gpsimd.memset(key[:, E:E + K], SENTINEL).then_inc(zeroed, 1)
            pool.wait_ge(zeroed, 2)
            for j in range(G):
                nc.gpsimd.memset(v_heads[j * S:(j + 1) * S, :, :, j, HD], 1.0).then_inc(zeroed, 1)
            pool.wait_ge(zeroed, 2 + G)

            pool.wait_ge(powers_set, 2)

            def inverse_sqrt(n):
                pool.wait_ge(var_ready, n + 1)
                nc.gpsimd.tensor_tensor(rstd[:, n:n + 1], var_eps[:, n:n + 1], inv_sqrt_power[:], ALU.pow
                                        ).then_inc(rstd_ready, 1)

            inverse_sqrt(0)

            def gu_low(p, slot, raw, c):
                pool.wait_ge(gu_hi_ready, p + 1)
                nc.gpsimd.tensor_tensor(gu_w[:, slot, 1, c * GU:(c + 1) * GU],
                                        gu_raw[:, bass.ds(raw * (DC * GU) + c * GU, GU)],
                                        gu_w[:, slot, 0, c * GU:(c + 1) * GU], ALU.subtract
                                        ).then_inc(gu_lo_ready[c], 1)

            for p in range(RING + 1):
                if p == 1:
                    inverse_sqrt(1)
                for c in range(DC):
                    gu_low(p, (p - 1) % (RING + 1), p or RAW, c)
            inverse_sqrt(2)
            for p in range(RING + 1, RAW):
                gu_low(p, (p - 1) % RING, p, 0)
            with nc.gpsimd.Fori(0, (PAIRS - RAW) // RING) as i:
                for u in range(RING):
                    gu_low(i * RING + (RAW + u), (u - 1) % RING, i * RING + u, 0)

        @block.tensor
        def _(pe):
            def merge_lora(m, bank):
                for c in range(DC):
                    last = nc.tensor.matmul(bank[:, c * D:(c + 1) * D], lora_sb[:, 0, m, c * 128:(c + 1) * 128],
                                            lora_sb[:, 1, m, :], start=True, stop=True)
                last.then_inc(lora_psum, 1)

            def transpose_xn(n):
                for c in range(DC):
                    pe.wait_ge(xn_ready, DC * n + c + 1)
                    nc.tensor.transpose(bXT[n][c][:, 0:T], xn[:, n, c * 128:(c + 1) * 128], ident
                                        ).then_inc(xnT_psum, 1)

            def project_T(banks, w, a, done):
                for k in range(DC):
                    pe.wait_ge(xnT_ready, DC * a + k + 1)
                    for c in range(DC):
                        last = nc.tensor.matmul(banks[c][:, 0:T], w[:, k, c * 128:(c + 1) * 128], xnT[:, a, k, :],
                                                start=(k == 0), stop=(k == DC - 1))
                        if k == DC - 1:
                            last.then_inc(done, 1)

            def keep_warm(bank, n):
                for _ in range(n):
                    nc.tensor.matmul(bank[:, :], warm_sb[:, 0:128], warm_sb[:, :], start=True, stop=True)

            def values(bank, x_t, w, chunks, batches):
                for b in batches:
                    for k in range(chunks):
                        for j in range(G):
                            last = nc.tensor.matmul(
                                bank[j * S:(j + 1) * S, b * NG * HD:(b + 1) * NG * HD],
                                x_t(k)[:, b * S:(b + 1) * S],
                                w(k).rearrange("p (n j d) -> p n j d", j=G, d=HD)[:, :, j, :],
                                start=(k == 0), stop=(k == chunks - 1), skip_group_check=True)
                last.then_inc(v_psum, 1)

            def scores(a, g):
                r = slice(64 * g, 64 * g + 64)
                if a == 0:
                    nc.tensor.matmul(bS[g][:, 0:2 * G * S], causal_sb[:, 0:128], causal_sb[:, 128:],
                                     start=True, stop=False, skip_group_check=True)
                for c in range(DC):
                    for b in range(B):
                        last = nc.tensor.matmul(bS[g][b * S:(b + 1) * S, c * G * S:(c + 1) * G * S],
                                                qT[r, a, c, b * S:(b + 1) * S],
                                                k_heads[r, c, :, b * S:(b + 1) * S],
                                                start=(a == 1), stop=True, skip_group_check=True)
                last.then_inc(scores_ready, 1)

            def transpose_probs(a, g):
                pe.wait_ge(exp_ready, 2 * a + g + 1)
                for c in range(DC):
                    last = nc.tensor.transpose((bT, bK)[g][:, c * T:(c + 1) * T],
                                               probs[:, g, c * G * S:(c + 1) * G * S], ident)
                last.then_inc(probsT_psum, 1)

            def attend(a, g):
                pe.wait_ge(probsT_ready, 2 * a + g + 1)
                for c in range(DC):
                    n = 2 * c + g
                    for b in range(B):
                        last = nc.tensor.matmul(bO[b * S:(b + 1) * S, n * G * V1:(n + 1) * G * V1],
                                                probsT[:, g, c, b * S:(b + 1) * S], v_heads[:, b, n],
                                                start=True, stop=True, skip_group_check=True)
                last.then_inc(pv_ready, 1)

            def residual(a, src):
                nc.tensor.matmul(bY[:, 0:D], ident, src, start=True, stop=False)

            def project_out(a, w):
                for c in range(DC):
                    pe.wait_ge(heads_ready, DC * a + c + 1)
                    nc.tensor.transpose(bHT[c][:, 0:T], heads_out[:, a, c * 128:(c + 1) * 128], ident
                                        ).then_inc(headsT_psum, 1)
                if a == 1:
                    pe.wait_ge(ld["rows"], 16)
                    nc.tensor.matmul(bY[:, 0:D], rows_sb[:, ONES:ONES + T], rows_sb[:, BO:BO + D],
                                     start=False, stop=False)
                keep_warm(bS0, WARM[11 + a])
                for c in range(DC):
                    pe.wait_ge(headsT_ready, DC * a + c + 1)
                    last = nc.tensor.matmul(bY[:, 0:D], heads_outT[:, a, c, :], w[:, c, :],
                                            start=False, stop=(c == DC - 1))
                last.then_inc(y_psum, 1)

            pe.wait_ge(warm_set, 1)
            keep_warm(bS0, WARM[0])
            pe.wait_ge(ld["small"], 16)
            transpose_xn(0)
            pe.wait_ge(ld["ctx"], 16)
            for c in range(DC):
                nc.tensor.matmul(bKK[c][:, 0:T], ctx_sb[:, WKV + c * 128:WKV + (c + 1) * 128],
                                 ctx_sb[:, CTX:CTX + T], start=True, stop=True).then_inc(k_psum, 1)
            keep_warm(bS0, WARM[1])
            pe.wait_ge(ld["xwq"], 16)
            project_T((bQ, bS1), xwq_sb, 0, q_psum)
            values(bV, lambda k: ctx_sb[:, CTX:CTX + T], lambda k: ctx_sb[:, WKV + D:WKV + 2 * D], 1, range(B))
            keep_warm(bO, WARM[2])
            pe.wait_ge(ld["causal"], 16)
            pe.wait_ge(q_ready, 2)
            pe.wait_ge(k_ready, 2)
            scores(0, 0)
            scores(0, 1)
            pe.wait_ge(ld["lora"], 16)
            merge_lora(0, bQ)
            keep_warm(bO, WARM[3])
            transpose_probs(0, 0)
            pe.wait_ge(ld["x"], 16)
            residual(0, x_sb[:])
            transpose_probs(0, 1)
            keep_warm(bS0, WARM[4])
            pe.wait_ge(v_ready, 2)
            attend(0, 0)
            attend(0, 1)
            merge_lora(1, bV)
            keep_warm(bS0, WARM[5])
            pe.wait_ge(ld["xwo"], 16)
            project_out(0, xwo_sb)
            pe.wait_ge(lora_merged, 1)
            merge_lora(2, bQ)
            merge_lora(3, bO)
            keep_warm(bS0, WARM[6])

            transpose_xn(1)
            keep_warm(bS0, WARM[7])
            aw = [aw_sb[:, m].rearrange("p (c n) -> p c n", c=DC) for m in range(4)]
            pe.wait_ge(x_ready, 1)
            project_T(bKK, aw[0], 1, k_psum)
            pe.wait_ge(lora_merged, 3)
            project_T((bQ, bS1), aw[1], 1, q_psum)
            values(bV, lambda k: xnT[:, 1, k, :], lambda k: aw[2][:, k, :], DC, range(B // 2))
            pe.wait_ge(q_ready, 4)
            pe.wait_ge(k_ready, 4)
            scores(1, 0)
            scores(1, 1)
            values(bQ, lambda k: xnT[:, 1, k, :], lambda k: aw[2][:, k, :], DC, range(B // 2, B))
            keep_warm(bO, WARM[8])
            transpose_probs(1, 0)
            residual(1, x1[:])
            transpose_probs(1, 1)
            pe.wait_ge(v_ready, 4)
            pe.wait_ge(lora_merged, 4)
            attend(1, 0)
            attend(1, 1)
            for c in range(DC):
                nc.tensor.matmul(bY[:, 0:D], small_sb[:, BIASV + c:BIASV + c + 1].to_broadcast([128, T]),
                                 aw[3][:, c, :], start=False, stop=False)
            keep_warm(bS0, WARM[9])
            project_out(1, aw[3])
            keep_warm(bS0, WARM[10])

            transpose_xn(2)
            keep_warm(bS0, WARM[13])
            for k in range(DC):
                pe.wait_ge(xnT_ready, 2 * DC + k + 1)
                last = nc.tensor.matmul(bQ[:, 0:E], xnT[:, 2, k, :], small_sb[:, ROUTER + k * E:ROUTER + (k + 1) * E],
                                        start=(k == 0), stop=(k == DC - 1))
            last.then_inc(logits_ready, 1)

            def gate_up(n, j):
                if not (isinstance(n, int) and n <= 3):
                    pe.wait_ge(clip_ready, n - 3)
                slot = RING if isinstance(n, int) and n == 1 else (j - 2) % RING
                for k in range(DC):
                    pe.wait_ge(gu_lo_ready[k], n)
                    for a, w in HI_LO:
                        last = nc.tensor.matmul(bGU[j][:, 0:GU], xnT_parts[:, a, k, :],
                                                gu_w[:, slot, w, k * GU:(k + 1) * GU],
                                                start=(k == 0 and a == w == 0), stop=(k == DC - 1 and a == 1))
                last.then_inc(gu_ready, 1)

            def transpose_h(n, j, width=2):
                pe.wait_ge(h_ready, n + 1)
                for e in range(width):
                    last = nc.tensor.transpose(bH[j % 2][:, e * T:(e + 1) * T], h[:, j % 2, e, :], ident)
                last.then_inc(hT_psum, 1)

            def down(n, j, visit, stop=False):
                pe.wait_ge(ld_dn[(j + 1) % 2], visit * 16)
                pe.wait_ge(hT_ready, n + 1)
                for e in range(2):
                    last = nc.tensor.matmul(bO[:, 0:D], hT[:, j % 2, e, :],
                                            dn_w[:, bass.ds((n - 1) * (2 * D) + e * D, D)],
                                            start=False, stop=(stop and e == 1), skip_group_check=True)
                last.then_inc(y_done, 1)

            pe.wait_ge(ld["shared"], 16)
            for k in range(DC):
                last = nc.tensor.matmul(bV[:, 0:2 * I], xnT[:, 2, k, :], shared_sb[:, k * 2 * I:(k + 1) * 2 * I],
                                        start=(k == 0), stop=(k == DC - 1))
            last.then_inc(gu_ready, 1)
            pe.wait_ge(xnT_parts_ready, 1)
            for n in range(1, 6):
                gate_up(n, n % 4)
            transpose_h(0, 0, width=1)
            transpose_h(1, 1)
            gate_up(6, 2)
            pe.wait_ge(hT_ready, 1)
            nc.tensor.matmul(bO[:, 0:D], hT[:, 0, 0, :], shared_sb[:, DC * 2 * I:], start=True, stop=False,
                             skip_group_check=True).then_inc(y_done, 1)
            transpose_h(2, 2)
            down(1, 1, 1)
            with nc.tensor.Fori(0, (PAIRS - RAW) // 4) as i:
                for u in range(3, 7):
                    gate_up(i * 4 + (u + 4), u % 4)
                    transpose_h(i * 4 + u, u % 4)
                    down(i * 4 + (u - 1), (u - 1) % 4, i * 2 + u // 2)
            for n in range(PAIRS - 5, PAIRS + 1):
                if n + 4 <= PAIRS:
                    gate_up(n + 4, n % 4)
                transpose_h(n, n % 4)
                down(n - 1, (n - 1) % 4, n // 2)
            down(PAIRS, 0, PAIRS // 2, stop=True)

        @block.scalar
        def _(act):
            act.dma_start(ctx_sb[:], ctx_kv).then_inc(ld["ctx"], 16)
            act.dma_start(xwq_sb[:], x_wq).then_inc(ld["xwq"], 16)
            nc.scalar.preload_act_table_set("natural_log_exp_and_others")

            def exp_half(a, g):
                act.wait_ge(shift_ready, 2 * a + g + 1)
                nc.scalar.activation(probs[:, g], shifted[:, g], ACT.Exp, scale=SM_SCALE).then_inc(exp_ready, 1)

            def copy_xnT(n):
                for c in range(DC):
                    act.wait_ge(xnT_psum, DC * n + c + 1)
                    nc.scalar.activation(xnT[:, n, c], bXT[n][c][:, 0:T], ACT.Copy).then_inc(xnT_ready, 1)

            def copy_v(a, heads, batches, bank):
                for j in heads:
                    r = slice(j * S, (j + 1) * S)
                    cols = slice(batches.start * NG * HD, batches.stop * NG * HD)
                    last = nc.scalar.activation(v_heads[r, batches.start:batches.stop, :, j, 0:HD],
                                                bank[r, cols].rearrange("p (b n d) -> p b n d", n=NG, d=HD), ACT.Copy)
                return last

            def gu_high(p, slot, raw, visit):
                act.wait_ge(ld_gu[0 if slot == RING else (slot + 1) % 2], visit * 16)
                if not (isinstance(p, int) and p <= RING):
                    act.wait_ge(gu_ready, p - 2)
                nc.scalar.activation(gu_w[:, slot, 0], gu_raw[:, bass.ds(raw * (DC * GU), DC * GU)], ACT.Copy
                                     ).then_inc(gu_hi_ready, 1)

            def copy_headsT(a):
                for c in range(DC):
                    act.wait_ge(headsT_psum, DC * a + c + 1)
                    nc.scalar.activation(heads_outT[:, a, c], bHT[c][:, 0:T], ACT.Copy).then_inc(headsT_ready, 1)

            act.wait_ge(zeroed, 2 + G)
            copy_xnT(0)
            for c in range(DC):
                act.wait_ge(q_psum, c + 1)
                nc.scalar.activation(qT[:, 0, c], (bQ, bS1)[c][:, 0:T], ACT.Copy).then_inc(q_ready, 1)
            act.wait_ge(v_psum, 1)
            copy_v(0, (0, 1, 2), range(B), bV).then_inc(v_ready, 1)
            exp_half(0, 0)
            exp_half(0, 1)
            gu_high(0, RING, RAW, 1)
            copy_headsT(0)
            gu_high(1, 0, 1, 1)
            gu_high(2, 1, 2, 2)

            copy_xnT(1)
            gu_high(3, 2, 3, 2)
            for c in range(DC):
                act.wait_ge(q_psum, DC + c + 1)
                nc.scalar.activation(qT[:, 1, c], (bQ, bS1)[c][:, 0:T], ACT.Identity,
                                     bias=small_sb[:, BIASQ + c:BIASQ + c + 1]).then_inc(q_ready, 1)
            act.wait_ge(v_psum, 2)
            copy_v(1, (0, 1, 2), range(B // 2), bV)
            exp_half(1, 0)
            act.wait_ge(v_psum, 3)
            copy_v(1, (0,), range(B // 2, B), bQ)
            exp_half(1, 1)
            copy_v(1, (1, 2), range(B // 2, B), bQ).then_inc(v_ready, 1)
            gu_high(4, 3, 4, 3)
            copy_headsT(1)

            copy_xnT(2)
            act.wait_ge(xnT_ready, 3 * DC)
            nc.scalar.activation(xnT_parts[:, 0], xnT[:, 2], ACT.Copy).then_inc(xnT_hi_ready, 1)
            act.wait_ge(logits_ready, 1)
            nc.scalar.activation(abs_logits[:], bQ[:, 0:E], ACT.Abs).then_inc(abs_ready, 1)
            act.wait_ge(abs_ready, 1)
            nc.scalar.activation(e_abs[:], abs_logits[:], ACT.Exp, scale=-1.0).then_inc(e_abs_ready, 1)
            act.wait_ge(one_plus_ready, 1)
            nc.scalar.activation(ln_one_plus[:], one_plus[:], ACT.Ln).then_inc(ln_ready, 1)
            act.wait_ge(softplus_ready, 1)
            act.wait_ge(powers_set, 2)
            nc.scalar.activation(ln_softplus[:], softplus[:], ACT.Ln, bias=ln_floor[:]
                                 ).then_inc(ln_softplus_ready, 1)
            act.wait_ge(half_power_ready, 1)
            nc.scalar.activation(root[:], half_power[:], ACT.Exp, scale=0.5).then_inc(root_ready, 1)
            nc.scalar.preload_act_table(ACT.Silu)

            def silu_unit(n, j, width=2):
                act.wait_ge(clip_ready, n + 1)
                nc.scalar.activation(silu[:, j % 2, 0:width], gu_clip[:, j, 0:width, 0, :], ACT.Silu
                                     ).then_inc(silu_ready, 1)

            def hT_unit(n, j, width=2):
                act.wait_ge(hT_psum, n + 1)
                nc.scalar.activation(hT[:, j, 0:width], bH[j][:, 0:width * T], ACT.Copy).then_inc(hT_ready, 1)

            silu_unit(0, 0, width=1)
            silu_unit(1, 1)
            gu_high(5, 0, 5, 3)
            hT_unit(0, 0, width=1)
            for n in (1, 2):
                silu_unit(n + 1, (n + 1) % 4)
                gu_high(n + 5, (n + 4) % RING, n + 5, (n + 5) // 2 + 1)
                hT_unit(n, n % 2)
            with nc.scalar.Fori(0, (PAIRS - RAW) // RING) as i:
                for u in range(RING):
                    silu_unit(i * RING + (4 + u), u)
                    gu_high(i * RING + (RAW + u), (u - 1) % RING, i * RING + u, i * (RING // 2) + (RAW + u) // 2 + 1)
                    hT_unit(i * RING + (3 + u), (3 + u) % 2)
            for n in range(PAIRS - 5, PAIRS):
                silu_unit(n + 1, (n + 1) % 4)
                hT_unit(n, n % 2)
            hT_unit(PAIRS, 0)

        @block.vector
        def _(dve):
            links = {"ln": 0, "route": 0}

            def link(ins, which, s):
                links[which] += 1
                ins.then_inc(s, 1)
                dve.wait_ge(s, links[which])

            def layer_norm(n, src):
                link(nc.vector.bn_stats(stats[:, n], src), "ln", ln_step)
                link(nc.vector.bn_aggr(moments[:, n], stats[:, n]), "ln", ln_step)
                nc.vector.tensor_scalar(var_eps[:, n:n + 1], moments[:, n, 1:2], EPS, None, ALU.add
                                        ).then_inc(var_ready, 1)
                if n == 0:
                    dve.wait_ge(ld["small"], 16)
                dve.wait_ge(rstd_ready, n + 1)
                for c in range(DC):
                    half = slice(c * 128, (c + 1) * 128)
                    nc.vector.tensor_scalar(xn[:, n, half], src[:, half], moments[:, n, 0:1], rstd[:, n:n + 1],
                                            ALU.subtract, ALU.mult).then_inc(xn_ready, 1)

            def spread_keys(a, c):
                dve.wait_ge(k_psum, DC * a + c + 1)
                src = bKK[c][:, 0:T].unsqueeze(1).to_broadcast([128, G, T])
                mask = hmask.unsqueeze(2).to_broadcast([128, G, T])
                if a == 0:
                    ins = nc.vector.tensor_tensor(k_heads[:, c], src, mask, ALU.mult)
                else:
                    ins = nc.vector.scalar_tensor_tensor(k_heads[:, c], src, small_sb[:, BIASK + c:BIASK + c + 1],
                                                         mask, ALU.add, ALU.mult)
                ins.then_inc(k_ready, 1)

            def shift_half(a, g):
                dve.wait_ge(scores_ready, 2 * a + g + 1)
                sc = bS[g][:, 0:2 * G * S].rearrange("p (h k) -> p h k", k=S)
                nc.vector.tensor_reduce(row_max[:, a, g], sc, AX_X, ALU.max).then_inc(max_ready, 1)
                dve.wait_ge(max_ready, 2 * a + g + 1)
                nc.vector.tensor_tensor(shifted[:, g].rearrange("p (h k) -> p h k", k=S), sc,
                                        row_max[:, a, g].unsqueeze(2).to_broadcast([T, 2 * G, S]), ALU.subtract
                                        ).then_inc(shift_ready, 1)

            def copy_probsT(a, g):
                dve.wait_ge(probsT_psum, 2 * a + g + 1)
                nc.vector.tensor_copy(probsT[:, g], (bT, bK)[g][:, 0:DC * T]).then_inc(probsT_ready, 1)

            def copy_v(a, batches, bank):
                j = G - 1
                r = slice(j * S, (j + 1) * S)
                cols = slice(batches.start * NG * HD, batches.stop * NG * HD)
                return nc.vector.tensor_copy(v_heads[r, batches.start:batches.stop, :, j, 0:HD],
                                             bank[r, cols].rearrange("p (b n d) -> p b n d", n=NG, d=HD))

            def merge_lora(m, bank):
                dve.wait_ge(lora_psum, m + 1)
                nc.vector.scalar_tensor_tensor(aw_sb[:, m], bank[:, :], LORA_SCALE, aw_sb[:, m],
                                               ALU.mult, ALU.add).then_inc(lora_merged, 1)

            def attention_tail(a, dst):
                dve.wait_ge(pv_ready, 2 * (a + 1))
                o = bO[:, 0:NH * V1].rearrange("p (h d) -> p h d", h=NH)
                nc.vector.reciprocal(inv_sum[:, a], o[:, :, HD]).then_inc(inv_ready, 1)
                dve.wait_ge(inv_ready, a + 1)
                for c in range(DC):
                    hs = slice(c * NH // 2, (c + 1) * NH // 2)
                    nc.vector.tensor_tensor(
                        heads_out[:, a, c * 128:(c + 1) * 128].rearrange("p (h d) -> p h d", d=HD), o[:, hs, 0:HD],
                        inv_sum[:, a, hs].unsqueeze(2).to_broadcast([T, NH // 2, HD]), ALU.mult
                        ).then_inc(heads_ready, 1)
                if a == 0:
                    merge_lora(1, bV)
                dve.wait_ge(y_psum, a + 1)
                layer_norm(a + 1, bY[:, 0:D])
                nc.vector.tensor_copy(dst, bY[:, 0:D]).then_inc(x_ready, 1)

            nc.vector.memset(warm_sb[:], 1.0).then_inc(warm_set, 1)
            dve.wait_ge(ld["x"], 16)
            layer_norm(0, x_sb[:])
            for c in range(DC):
                spread_keys(0, c)
            for a in range(2):
                if a == 1:
                    merge_lora(2, bQ)
                    merge_lora(3, bO)
                    for c in range(DC):
                        spread_keys(1, c)
                if a == 1:
                    dve.wait_ge(v_psum, 2)
                    copy_v(1, range(B // 2), bV)
                shift_half(a, 0)
                shift_half(a, 1)
                dve.wait_ge(v_psum, (1, 3)[a])
                if a == 0:
                    dve.wait_ge(zeroed, 2 + G)
                copy_v(a, (range(B), range(B // 2, B))[a], (bV, bQ)[a]).then_inc(v_ready, 1)
                copy_probsT(a, 0)
                copy_probsT(a, 1)
                if a == 0:
                    dve.wait_ge(ld["aw"], 16)
                    merge_lora(0, bQ)
                attention_tail(a, (x1[:], x2[:])[a])
            dve.wait_ge(xnT_hi_ready, 1)
            nc.vector.tensor_tensor(xnT_parts[:, 1], xnT[:, 2], xnT_parts[:, 0], ALU.subtract
                                    ).then_inc(xnT_parts_ready, 1)

            def clip(n, j, width=2, bank=None):
                dve.wait_ge(gu_ready, n + 1)
                if not (isinstance(n, int) and n < 4):
                    dve.wait_ge(h_ready, n - 3)
                nc.vector.tensor_scalar(gu_clip[:, j, 0:width], (bank or bGU[j])[:, 0:width * 2 * I], CLIP, -CLIP,
                                        ALU.min, ALU.max).then_inc(clip_ready, 1)

            def step(ins):
                link(ins, "route", route_step)

            logits = bQ[:, 0:E]
            dve.wait_ge(e_abs_ready, 1)
            nc.vector.tensor_scalar(one_plus[:], e_abs[:], 1.0, None, ALU.add).then_inc(one_plus_ready, 1)
            dve.wait_ge(one_plus_ready, 1)
            step(nc.vector.tensor_scalar(den[:], one_plus[:], -1.0, TINY, ALU.add, ALU.add))
            step(nc.vector.reciprocal(den[:], den[:]))
            step(nc.vector.tensor_tensor(den[:], den[:], e_abs[:], ALU.mult))
            dve.wait_ge(ln_ready, 1)
            step(nc.vector.scalar_tensor_tensor(ratio[:], ln_one_plus[:], TINY, den[:], ALU.add, ALU.mult))
            nc.vector.scalar_tensor_tensor(softplus[:], logits, 0.0, ratio[:], ALU.max, ALU.add
                                           ).then_inc(softplus_ready, 1)
            dve.wait_ge(ln_softplus_ready, 1)
            nc.vector.scalar_tensor_tensor(half_power[:], logits, -100.0, ln_softplus[:], ALU.max, ALU.min
                                           ).then_inc(half_power_ready, 1)
            clip(0, 0, width=1, bank=bV)
            dve.wait_ge(root_ready, 1)
            step(nc.vector.reciprocal(inv_root[:], root[:]))
            step(nc.vector.tensor_tensor(inv_root[:], inv_root[:], softplus[:], ALU.mult))
            step(nc.vector.tensor_tensor(score2[:], inv_root[:], root[:], ALU.add))
            dve.wait_ge(zeroed, 2)
            step(nc.vector.scalar_tensor_tensor(key[:, 0:E], score2[:], 0.5, small_sb[:, EBIAS:EBIAS + E],
                                                ALU.mult, ALU.add))
            clip(1, 1)
            step(nc.vector.max(top8[:], key[:, 0:E]))
            step(nc.vector.memset(top8[:, K:8], SENTINEL))
            step(nc.vector.match_replace(replaced[:], top8[:], key[:], -SENTINEL))
            step(nc.vector.tensor_tensor(chosen[:], replaced[:, 0:E], key[:, 0:E], ALU.not_equal))
            step(nc.vector.scalar_tensor_tensor(weight[:], chosen[:], 0.5, score2[:], ALU.mult, ALU.mult,
                                                accum_out=weight_sum[:, 0:1]))
            step(nc.vector.tensor_scalar(weight_sum[:, 1:2], weight_sum[:, 0:1], 1e-20, None, ALU.add))
            step(nc.vector.reciprocal(weight_sum[:, 0:1], weight_sum[:, 1:2]))
            nc.vector.tensor_scalar(gate[:], weight[:], weight_sum[:, 0:1], None, ALU.mult).then_inc(gate_ready, 1)

            def gu_low(p, slot, raw):
                dve.wait_ge(gu_hi_ready, p + 1)
                nc.vector.tensor_tensor(gu_w[:, slot, 1, GU:], gu_raw[:, bass.ds(raw * (DC * GU) + GU, GU)],
                                        gu_w[:, slot, 0, GU:], ALU.subtract).then_inc(gu_lo_ready[1], 1)

            def gate_h(n, j):
                dve.wait_ge(silu_ready, n + 1)
                if not (isinstance(n, int) and n < 2):
                    dve.wait_ge(hT_psum, n - 1)
                for e in range(2):
                    last = nc.vector.scalar_tensor_tensor(h[:, j % 2, e], gu_clip[:, j, e, 1, :],
                                                          gate[:, bass.ds((n - 1) * 2 + e, 1)], silu[:, j % 2, e],
                                                          ALU.mult, ALU.mult)
                last.then_inc(h_ready, 1)

            dve.wait_ge(silu_ready, 1)
            nc.vector.tensor_tensor(h[:, 0, 0], gu_clip[:, 0, 0, 1, :], silu[:, 0, 0], ALU.mult).then_inc(h_ready, 1)
            dve.wait_ge(gate_ready, 1)
            for n in range(1, 4):
                if n == 1:
                    gate_h(1, 1)
                clip(n + 1, (n + 1) % 4)
                if n > 1:
                    gate_h(n, n % 4)
                gu_low(n + 4, (n + 3) % RING, n + 4)
            with nc.vector.Fori(0, (PAIRS - RAW) // RING) as i:
                for u in range(RING):
                    clip(i * RING + (5 + u), (5 + u) % 4)
                    gate_h(i * RING + (4 + u), u)
                    gu_low(i * RING + (RAW + u), (u - 1) % RING, i * RING + u)
            for n in range(PAIRS - 4, PAIRS):
                clip(n + 1, (n + 1) % 4)
                gate_h(n, n % 4)
            gate_h(PAIRS, 0)
            dve.wait_ge(y_done, PAIRS + 1)
            nc.vector.tensor_tensor(y_sb[:], bO[:, 0:D], x2[:], ALU.add).then_inc(fin, 1)


def kernel(**inputs):
    import ml_dtypes
    import numpy as np
    import concourse.bacc as bacc
    from concourse.bass_utils import run_bass_kernel_spmd

    v = {n: np.asarray(a) for n, a in inputs.items()}

    def chunked(w):
        return w.T.reshape(DC, 128, w.shape[0]).transpose(1, 0, 2)

    small = np.zeros((128, SMALL), np.float32)
    small[:, IDENT:IDENT + 128] = np.eye(128, dtype=np.float32)
    small[:, HMASK:HMASK + G] = np.arange(128)[:, None] // HD % G == np.arange(G)[None, :]
    small[:, BIASV:BIASV + DC] = v["L0_attn_bv"].reshape(DC, 128).T
    small[:, BIASQ:BIASQ + DC] = v["L0_attn_bq"].reshape(DC, 128).T
    small[:, BIASK:BIASK + DC] = v["L0_attn_bk"].reshape(DC, 128).T
    small[:, EBIAS:EBIAS + E] = v["L0_ffn_expert_bias"][None, :]
    small[:, ROUTER:] = chunked(v["L0_ffn_router_w"]).reshape(128, DC * E)

    causal = np.zeros((128, 128 + 2 * G * S), np.float32)
    causal[:, 0:128] = np.eye(128)
    hidden = np.arange(S)[None, :] > (np.arange(T) % S)[:, None]
    causal[:, 128:] = np.tile(np.where(hidden, -1e30, 0.0), (1, 2 * G))
    causal = causal.astype(ml_dtypes.bfloat16)

    ctx_kv = np.concatenate([v["ctx_512"][:, :S].reshape(T, L).T, v["L0_xattn_Wkv_expand"].T], axis=1)
    lora = np.stack([np.stack([v["L0_attn_B" + m] for m in "kqvo"], axis=1),
                     np.stack([v["L0_attn_A" + m].T for m in "kqvo"], axis=1)], axis=1)
    rows = np.concatenate([np.ones(T, np.float32), v["L0_attn_bo"]])[None, :]
    attn_w = np.stack([chunked(v["L0_attn_W" + m]).reshape(128, DC * D) for m in "kqvo"], axis=1)

    shared_gu = np.concatenate([chunked(v["L0_ffn_shared_gate_w"]), chunked(v["L0_ffn_shared_up_w"])], axis=2)
    shared = np.concatenate([shared_gu.reshape(128, -1), v["L0_ffn_shared_down_w"].T], axis=1)
    gu = np.stack([v["L0_ffn_gate_w"], v["L0_ffn_up_w"]], axis=1)
    gu = gu.reshape(PAIRS, GU, DC, 128).transpose(3, 0, 2, 1).reshape(128, PAIRS, DC * GU)
    dn = v["L0_ffn_down_w"].transpose(2, 0, 1).reshape(128, PAIRS, 2 * D)
    moe = np.concatenate([gu, dn], axis=2).reshape(128, -1)

    arrays = {"x": v["x"].reshape(T, D), "small": small, "causal": causal, "ctx_kv": ctx_kv,
              "x_wq": chunked(v["L0_xattn_Wq"]), "x_wo": chunked(v["L0_xattn_Wout"]), "lora": lora, "rows": rows,
              "attn_w": attn_w, "shared_w": shared, "moe_w": moe}
    arrays = {n: np.ascontiguousarray(a) for n, a in arrays.items()}

    nc = bacc.Bacc("TRN2", target_bir_lowering=False, num_devices=1)
    args = {n: nc.dram_tensor(n + "_dram", a.shape, mybir.dt.from_np(a.dtype), kind="ExternalInput").ap()
            for n, a in arrays.items()}
    out = nc.dram_tensor("out_dram", (T, D), F32, kind="ExternalOutput").ap()
    build(nc, out=out, **args)
    r = run_bass_kernel_spmd(nc, [{n + "_dram": a for n, a in arrays.items()}], core_ids=[0])
    return r.results[0]["out_dram"].reshape(B, S, D)
```
